# Optimizing a Trainium2 kernel written in Bass

```python
import numpy as np
import jax
import jax.numpy as jnp

def _softmax(x, axis=-1):
    return jax.nn.softmax(x, axis=axis)

def _gelu(x):
    return jax.nn.gelu(x, approximate=True)

def _silu(x):
    return jax.nn.silu(x)

def _sigmoid(x):
    return jax.nn.sigmoid(x)

def _layernorm(x, axis=-1, eps=1e-05):
    m = jnp.mean(x, axis=axis, keepdims=True)
    v = jnp.var(x, axis=axis, keepdims=True)
    return (x - m) / jnp.sqrt(v + eps)

def _scatter_add(tgt, idx, src, axis=0):
    return tgt.at[idx].add(src)

def _segment_sum(src, seg, n):
    return jax.ops.segment_sum(src, seg, n)
kernel_name = 'mk_decoder_preln_d1_seqx_r8_05e152'

def setup_inputs(seed: int=0):
    np.random.seed(seed)
    _w = jnp.asarray

    def _rec_inputs():
        import jax
        import jax.numpy as jnp
        _rk = jax.random.key(seed)
        x = 7.22e-05 + 1 * jax.random.normal(jax.random.fold_in(_rk, 1), (32, 128, 128), jnp.float32)
        _lenS = 128 - jax.random.randint(jax.random.fold_in(_rk, 7), (32,), 0, max(1, 128 // 4) + 1, jnp.int32)
        _lenS2 = 128 - jax.random.randint(jax.random.fold_in(_rk, 8), (32,), 0, max(1, 128 // 4) + 1, jnp.int32)
        _ctx_1024P = jax.random.normal(jax.random.fold_in(_rk, 11), (32, 16, 128), jnp.float32)
        _ctx_1024c = jax.random.dirichlet(jax.random.fold_in(_rk, 511), 0.3 * jnp.ones((16,), jnp.float32), (32, 128))
        _ctx_1024t = jnp.einsum('bsk,bkd->bsd', _ctx_1024c, _ctx_1024P)
        _ctx_1024t = _ctx_1024t * jax.lax.rsqrt(jnp.mean(jnp.square(_ctx_1024t)) + 1e-12) * 0.953939
        ctx_1024 = 4.13588e-05 + 0.999923 * (_ctx_1024t + 0.3 * jax.random.normal(jax.random.fold_in(_rk, 611), (32, 128, 128), jnp.float32))
        return (x, ctx_1024)
    x, ctx_1024 = _rec_inputs()

    def _L0_attn_setup():
        import jax, jax.numpy as jnp
        import numpy as np
        import math
        DIM = 128
        NUM_HEADS = 16
        HEAD_DIM = DIM // NUM_HEADS
        WINDOW = 32

        def _apply_rotary(x, cos, sin):
            d = x.shape[-1] // 2
            x1, x2 = (x[..., :d], x[..., d:])
            return jnp.concatenate([x1 * cos - x2 * sin, x2 * cos + x1 * sin], axis=-1)
        key = jax.random.key(seed)
        k1, k2, k3 = jax.random.split(key, 3)
        B, T = (2, 256)
        x = jax.random.normal(k1, (B, T, DIM), dtype=jnp.float32)
        w_qkv = jax.random.normal(k2, (3 * DIM, DIM), dtype=jnp.float32) * (1.0 / math.sqrt(DIM))
        w_out = jax.random.normal(k3, (DIM, DIM), dtype=jnp.float32) * (1.0 / math.sqrt(DIM))
        return {'x': x, 'w_qkv': w_qkv, 'w_out': w_out}
    _L0_attn_all = _L0_attn_setup()
    _L0_attn_in = {k: v for k, v in _L0_attn_all.items() if k in ('w_qkv', 'w_out')}
    del _L0_attn_all

    def _L0_xattn_setup():
        import jax, jax.numpy as jnp
        import numpy as np
        B, S, D, H, W = (2, 512, 128, 16, 16)
        HD = D // H
        key = jax.random.key(seed)
        ks = jax.random.split(key, 10)
        std = 0.02
        mk_w = lambda k: jax.random.normal(k, (D, D), jnp.float32) * std
        mk_b = lambda k: jax.random.normal(k, (D,), jnp.float32) * std
        return {'query': jax.random.normal(ks[0], (B, S, D), jnp.float32), 'kv': jax.random.normal(ks[1], (B, S, D), jnp.float32), 'Wq': mk_w(ks[2]), 'bq': mk_b(ks[3]), 'Wk': mk_w(ks[4]), 'bk': mk_b(ks[5]), 'Wv': mk_w(ks[6]), 'bv': mk_b(ks[7]), 'Wo': mk_w(ks[8]), 'bo': mk_b(ks[9]), 'is_causal': 1}
    _L0_xattn_all = _L0_xattn_setup()
    _L0_xattn_in = {k: v for k, v in _L0_xattn_all.items() if k in ('Wq', 'bq', 'Wk', 'bk', 'Wv', 'bv', 'Wo', 'bo')}
    del _L0_xattn_all

    def _L0_ffn_setup():
        import jax, jax.numpy as jnp
        import numpy as np
        TOP_K = 2
        key = jax.random.key(seed)
        k0, k1, k2, k3 = jax.random.split(key, 4)
        B, T, C, E, F = (4, 256, 128, 8, 512)
        x = jax.random.normal(k0, (B, T, C), dtype=jnp.float32)
        gate_w = jax.random.normal(k1, (C, E), dtype=jnp.float32) * 0.02
        w1 = jax.random.normal(k2, (E, C, F), dtype=jnp.float32) * 0.02
        w2 = jax.random.normal(k3, (E, F, C), dtype=jnp.float32) * 0.02
        return {'x': x, 'gate_w': gate_w, 'w1': w1, 'w2': w2}
    _L0_ffn_all = _L0_ffn_setup()
    _L0_ffn_in = {k: v for k, v in _L0_ffn_all.items() if k in ('gate_w', 'w1', 'w2')}
    del _L0_ffn_all
    return {'x': x, 'ctx_1024': ctx_1024, 'L0_attn_w_qkv': _L0_attn_in['w_qkv'], 'L0_attn_w_out': _L0_attn_in['w_out'], 'L0_xattn_Wq': _L0_xattn_in['Wq'], 'L0_xattn_bq': _L0_xattn_in['bq'], 'L0_xattn_Wk': _L0_xattn_in['Wk'], 'L0_xattn_bk': _L0_xattn_in['bk'], 'L0_xattn_Wv': _L0_xattn_in['Wv'], 'L0_xattn_bv': _L0_xattn_in['bv'], 'L0_xattn_Wo': _L0_xattn_in['Wo'], 'L0_xattn_bo': _L0_xattn_in['bo'], 'L0_ffn_gate_w': _L0_ffn_in['gate_w'], 'L0_ffn_w1': _L0_ffn_in['w1'], 'L0_ffn_w2': _L0_ffn_in['w2']}

def reference(x, ctx_1024, L0_attn_w_qkv, L0_attn_w_out, L0_xattn_Wq, L0_xattn_bq, L0_xattn_Wk, L0_xattn_bk, L0_xattn_Wv, L0_xattn_bv, L0_xattn_Wo, L0_xattn_bo, L0_ffn_gate_w, L0_ffn_w1, L0_ffn_w2):
    import jax
    import jax.numpy as jnp

    def _L0_attn_ref(x, w_qkv, w_out):
        import jax, jax.numpy as jnp
        import numpy as np
        import math
        DIM = 128
        NUM_HEADS = 16
        HEAD_DIM = DIM // NUM_HEADS
        WINDOW = 32

        def _apply_rotary(x, cos, sin):
            d = x.shape[-1] // 2
            x1, x2 = (x[..., :d], x[..., d:])
            return jnp.concatenate([x1 * cos - x2 * sin, x2 * cos + x1 * sin], axis=-1)
        B, T, C = x.shape
        H, Dh = (NUM_HEADS, HEAD_DIM)
        qkv = (x @ w_qkv.T).reshape(B, T, 3, H, Dh)
        q, k, v = (qkv[:, :, 0], qkv[:, :, 1], qkv[:, :, 2])
        q = jnp.transpose(q, (0, 2, 1, 3))
        k = jnp.transpose(k, (0, 2, 1, 3))
        v = jnp.transpose(v, (0, 2, 1, 3))
        inv_freq = 1.0 / 10000.0 ** (jnp.arange(0, Dh, 2, dtype=jnp.float32) / Dh)
        t = jnp.arange(T, dtype=jnp.float32)
        freqs = jnp.einsum('i,j->ij', t, inv_freq)
        cos, sin = (jnp.cos(freqs), jnp.sin(freqs))
        q = _apply_rotary(q, cos, sin)
        k = _apply_rotary(k, cos, sin)
        scale = 1.0 / math.sqrt(Dh)
        attn = jnp.einsum('bhqd,bhkd->bhqk', q, k) * scale
        i = jnp.arange(T)[:, None]
        j = jnp.arange(T)[None, :]
        allowed = (j <= i) & (i - j < WINDOW)
        attn = jnp.where(allowed, attn, -jnp.inf)
        attn = jax.nn.softmax(attn, axis=-1)
        out = jnp.einsum('bhqk,bhkd->bhqd', attn, v)
        out = jnp.transpose(out, (0, 2, 1, 3)).reshape(B, T, C)
        return out @ w_out.T

    def _L0_xattn_ref(query, kv, Wq, bq, Wk, bk, Wv, bv, Wo, bo, is_causal):
        import jax, jax.numpy as jnp
        import numpy as np
        B, S, D, H, W = (2, 512, 128, 16, 16)
        HD = D // H
        b, s, d = query.shape

        def split_heads(x):
            return x.reshape(b, s, H, HD).transpose(0, 2, 1, 3)
        Q = split_heads(query @ Wq.T + bq)
        K = split_heads(kv @ Wk.T + bk)
        V = split_heads(kv @ Wv.T + bv)
        pad = W - 1
        Kp = jnp.pad(K, ((0, 0), (0, 0), (pad, 0), (0, 0)))
        Vp = jnp.pad(V, ((0, 0), (0, 0), (pad, 0), (0, 0)))
        idx = jnp.arange(s)[:, None] + jnp.arange(W)[None, :]
        Kw = Kp[:, :, idx]
        Vw = Vp[:, :, idx]
        scores = jnp.einsum('bhsd,bhswd->bhsw', Q, Kw) / np.sqrt(HD).astype(np.float32)
        if is_causal:
            mask = jnp.arange(W)[None, :] <= jnp.arange(s)[:, None]
            scores = jnp.where(mask[None, None], scores, -jnp.inf)
        attn = jax.nn.softmax(scores, axis=-1)
        out = jnp.einsum('bhsw,bhswd->bhsd', attn, Vw)
        out = out.transpose(0, 2, 1, 3).reshape(b, s, d)
        return out @ Wo.T + bo

    def _L0_ffn_ref(x, gate_w, w1, w2):
        import jax, jax.numpy as jnp
        import numpy as np
        TOP_K = 2
        E = gate_w.shape[-1]
        probs = jax.nn.softmax(x @ gate_w, axis=-1)
        topw, topi = jax.lax.top_k(probs, TOP_K)
        topw = topw / topw.sum(axis=-1, keepdims=True)
        combine = (jax.nn.one_hot(topi, E, dtype=x.dtype) * topw[..., None]).sum(axis=-2)

        def body(acc, params):
            w1_i, w2_i, cw = params
            h = jax.nn.gelu(x @ w1_i, approximate=False)
            return (acc + cw[..., None] * (h @ w2_i), None)
        acc0 = jnp.zeros_like(x)
        out, _ = jax.lax.scan(body, acc0, (w1, w2, jnp.moveaxis(combine, -1, 0)))
        return out
    x = x + _L0_attn_ref(_layernorm(x, axis=-1), L0_attn_w_qkv, L0_attn_w_out)
    x = x + _L0_xattn_ref(_layernorm(x, axis=-1), ctx_1024, L0_xattn_Wq, L0_xattn_bq, L0_xattn_Wk, L0_xattn_bk, L0_xattn_Wv, L0_xattn_bv, L0_xattn_Wo, L0_xattn_bo, 1)
    x = x + _L0_ffn_ref(_layernorm(x, axis=-1), L0_ffn_gate_w, L0_ffn_w1, L0_ffn_w2)
    return x

_drawn_inputs = setup_inputs


def setup_inputs(seed=0):
    import zlib

    import numpy as np

    out = dict(_drawn_inputs(seed))
    spreads = {}
    factors = {'L0_xattn_Wq': 8.0,
     'L0_xattn_bq': 64.0,
     'L0_xattn_Wk': 8.0,
     'L0_xattn_bk': 64.0,
     'L0_xattn_bv': 8.0}
    for name, (base, spread) in spreads.items():
        noise = np.random.default_rng([zlib.crc32(name.encode()), seed]).standard_normal(out[name].shape)
        drawn = base * np.exp(spread * noise) if base else spread * noise
        out[name] = jnp.asarray(drawn.astype(out[name].dtype))
    for name, factor in factors.items():
        out[name] = (out[name] * factor).astype(out[name].dtype)
    return out
```

```python
import math

import numpy as np

import concourse.bass as bass
from concourse import mybir

P = 128
B = 32
HEADS, HD = 16, 8
BLK = 32
NBLK = P // BLK
G = 4
NG = HEADS // G
WIN = 2 * BLK
PAIRS = HEADS // 2
VC = 2 * HD + 2
SELF_WINDOW, CROSS_WINDOW = 32, 16
SCALE = 1.0 / math.sqrt(HD)
EPS = 1e-5
MASKED = -1e30

E, F, TOPK = 8, 512, 2
FC = F // P
TOKENS = B * P
CAP = TOKENS + P
ROW = P + 4
SLOTS = (TOKENS * TOPK + E * (P - 1)) // P
U = 8
BLOCKS = -(-SLOTS // U) * U

C_IDENT = 0
C_COS = C_IDENT + P
C_SIN = C_COS + 2 * P
C_MASKS = C_SIN + 2 * P
C_HEAD = C_MASKS + 2 * WIN
C_GROUP = C_HEAD + G
C_BEFORE = C_GROUP + NG
C_IOTA = C_BEFORE + P
C_ROWNO = C_IOTA + E
C_REGION = C_ROWNO + 1
C_BLOCKNO = C_REGION + E
C_END = C_BLOCKNO + BLOCKS

KEYS_OF = [(0, None), (0, 1), (2, 1), (2, 3)]
BLOCK_ORDER = (0, 2, 1, 3)


def shape_constants():
    c = np.zeros((P, C_END), np.float32)
    c[:, C_IDENT:C_IDENT + P] = np.eye(P)
    inv = (1.0 / np.float32(10000.0) ** (np.arange(0, HD, 2, dtype=np.float32) / np.float32(HD))).astype(np.float32)
    ang = (np.arange(P, dtype=np.float32)[:, None] * inv[None, :]).astype(np.float32)
    cos, sin = np.cos(ang).astype(np.float32), np.sin(ang).astype(np.float32)
    feat = np.arange(P) % HD
    cosT = cos.T[feat % (HD // 2)]
    sinT = sin.T[feat % (HD // 2)] * np.where(feat < HD // 2, -1.0, 1.0)[:, None]
    order = np.concatenate([np.arange(b * BLK, (b + 1) * BLK) for b in BLOCK_ORDER])
    c[:, C_COS:C_COS + P], c[:, C_COS + P:C_COS + 2 * P] = cosT, cosT[:, order]
    c[:, C_SIN:C_SIN + P], c[:, C_SIN + P:C_SIN + 2 * P] = sinT, sinT[:, order]
    for q in range(P):
        for slot in range(2):
            block = KEYS_OF[q // BLK][slot]
            for k in range(BLK):
                if block is None:
                    own, cross = False, k < min(q + 1, CROSS_WINDOW - 1 - q)
                else:
                    key = block * BLK + k
                    own = key <= q and q - key < SELF_WINDOW
                    cross = key <= q and q - key < CROSS_WINDOW and key - (q - CROSS_WINDOW + 1) <= q
                for n, allowed in enumerate((own, cross)):
                    c[q, C_MASKS + n * WIN + slot * BLK + k] = 0.0 if allowed else MASKED
    for p in range(P):
        c[p, C_HEAD + (p // HD) % G] = 1.0
        c[p, C_GROUP + p // (G * HD)] = 1.0
        c[p, C_BEFORE + p + 1:C_BEFORE + P] = 1.0
        c[p, C_IOTA:C_IOTA + E] = np.arange(E)
        c[p, C_ROWNO] = p
        c[p, C_REGION:C_REGION + E] = np.arange(E) * CAP
        c[p, C_BLOCKNO:C_BLOCKNO + BLOCKS] = np.arange(BLOCKS)
    return c


def build(nc, x_in, ctxT_in, consts_in, wself_in, wcross_in, cols_in, rows_in, gate_in, w1_in, w2_in, out, parts=3):
    from contextlib import ExitStack
    F32, BF16, I32, U32 = mybir.dt.float32, mybir.dt.bfloat16, mybir.dt.int32, mybir.dt.uint32
    ALU, ACT, AX = mybir.AluOpType, mybir.ActivationFunctionType, mybir.AxisListType

    ctx = ExitStack()
    with ctx:
        def sb(name, shape, dt=F32):
            return ctx.enter_context(nc.sbuf_tensor(name, shape, dt))

        def pb(name):
            return ctx.enter_context(nc.psum_tensor(name, [P, 512], F32))

        def sem(name):
            return ctx.enter_context(nc.semaphore(name))

        sent = nc.dram_tensor("sent_rows", [(E + 1) * CAP, ROW], F32, kind="Internal").ap()
        results = nc.dram_tensor("expert_results", [TOPK * TOKENS, P], F32, kind="Internal").ap()

        x = sb("x", [P, B * P])
        consts = sb("consts", [P, C_END])
        wself = sb("wself", [P, 6 * P])
        wcross = sb("wcross", [P, 4 * P])
        cols = sb("cols", [P, 2])
        rows = sb("rows", [P, 2 * P])
        gate = sb("gate", [P, E])
        w1 = sb("w1", [P, E * F])
        w2 = sb("w2", [P, E * F])
        ident_bf = sb("ident_bf", [P, P], BF16)
        minus_ident_bf = sb("minus_ident_bf", [P, P], BF16)
        masks_bf = sb("masks_bf", [P, 2 * WIN], BF16)
        ones = sb("ones", [P, P])

        stats = sb("stats", [P, 6])
        mean_var = sb("mean_var", [P, 2])
        eps = sb("eps", [P, 1])
        minus_half = sb("minus_half", [P, 1])
        var_eps = sb("var_eps", [P, 1])
        rstd = sb("rstd", [P, 1])
        xn = sb("xn", [P, P])
        xnT = sb("xnT", [P, 2, P])
        ctxT = sb("ctxT", [P, 2, P])
        turned_cos = sb("turned_cos", [P, 2, P])
        turned_sin = sb("turned_sin", [P, 2, P])
        qk = sb("qk", [P, 2, P])
        q_groups = sb("q_groups", [P, NG, P])
        k_heads = sb("k_heads", [P, G, P + BLK])
        shift = sb("shift", [P, HEADS], BF16)
        probs = sb("probs", [P, HEADS * WIN])
        probsT = sb("probsT", [P, PAIRS, P])
        values = sb("values", [P, 2, NBLK, PAIRS, VC])
        inv_sum = sb("inv_sum", [P, PAIRS, 2])
        att = sb("att", [P, P])
        attT = sb("attT", [P, P])

        p_scores = [pb("p_scores0"), pb("p_scores1")]
        p_probsT = [pb("p_probsT0"), pb("p_probsT1")]
        p_qk, p_v, p_att, p_misc = pb("p_qk"), pb("p_v"), pb("p_att"), pb("p_misc")
        p_xT, p_attT, p_proj = p_misc[:, 0:P], p_misc[:, P:2 * P], p_misc[:, 2 * P:3 * P]

        row = sb("row", [P, 2, TOPK, ROW])
        xT_gate = sb("xT_gate", [P, P])
        logits = sb("logits", [P, E])
        top = sb("top", [P, 8])
        top_at = sb("top_at", [P, 8], U32)
        top_atf = sb("top_atf", [P, TOPK])
        ratio = sb("ratio", [P, 1])
        ratio1 = sb("ratio1", [P, 1])
        onehot = sb("onehot", [P, TOPK, E])
        begin = sb("begin", [P, 3, E])
        place = sb("place", [P, TOPK, E])
        mine = sb("mine", [P, TOPK, E])
        slot_f = sb("slot_f", [P, TOPK])
        slot_u = sb("slot_u", [P, 2, TOPK], U32)
        result_no = sb("result_no", [P, 2])
        pad_row = sb("pad_row", [P, ROW])
        pad_f = sb("pad_f", [P, E + 1])
        pad_u = sb("pad_u", [P, E + 1], U32)
        count_i = sb("count_i", [P, E], I32)
        nblocks_i = sb("nblocks_i", [P, E], I32)
        nblocks = sb("nblocks", [P, E])
        ends = sb("ends", [P, 4, E])
        skip = sb("skip", [P, E])
        past = sb("past", [P, BLOCKS, E])
        block_f = sb("block_f", [P, 2, BLOCKS])
        block_tab = sb("block_tab", [P, 2, BLOCKS], I32)
        p_logits, p_place, p_total = p_v[:, 0:E], p_att[:, 0:16], p_att[:, 16:32]

        got = sb("got", [P, U, ROW])
        gotT = sb("gotT", [P, P])
        hidden = sb("hidden", [P, F])
        hiddenT = sb("hiddenT", [P, FC, P])
        weighted = sb("weighted", [P, U, P])
        result_at = sb("result_at", [P, U], U32)
        p_gotT, p_hidden, p_hiddenT, p_y = p_misc[:, 0:P], p_scores[0], p_probsT[0], p_att[:, 0:P]

        CH = 4
        back = sb("back", [P, 2, TOPK, CH, P])

        s_x = [sem(f"x_loaded{i}") for i in range(2)]
        s_w = sem("weights_loaded")
        s_moe_w = sem("expert_weights_loaded")
        s_const = sem("constants_made")
        s_zero = sem("buffers_cleared")
        s_ctx = [sem(f"ctx_loaded{i}") for i in range(2)]
        s_stats, s_mv, s_ve, s_rstd = sem("stats_made"), sem("mean_var_made"), sem("var_eps_made"), sem("rstd_made")
        s_xn, s_xTraw, s_xT = sem("xn_made"), sem("xT_in_psum"), sem("xT_made")
        s_bo = sem("bo_added")
        s_qkraw, s_rot, s_qk = sem("qk_in_psum"), sem("rotary_parts"), sem("qk_made")
        s_spread = sem("qk_spread")
        s_scores, s_max, s_shifted = sem("scores_made"), sem("max_made"), sem("scores_shifted")
        s_probs, s_pTraw, s_pT = sem("probs_made"), sem("probsT_in_psum"), sem("probsT_made")
        s_vraw, s_v = sem("v_in_psum"), sem("v_made")
        s_attraw, s_inv, s_att = sem("att_in_psum"), sem("sums_inverted"), sem("att_made")
        s_aTraw, s_aT, s_proj, s_res = sem("attT_in_psum"), sem("attT_made"), sem("proj_in_psum"), sem("x_updated")

        s_twin, s_gate, s_route, s_ratio = sem("row_twin_made"), sem("gate_in_psum"), sem("route_steps"), sem("ratio_made")
        s_onehot, s_placed, s_slot = sem("onehot_made"), sem("places_in_psum"), sem("slots_made")
        s_sent = [sem(f"rows_sent{i}") for i in range(2)]
        s_pads, s_padsent, s_table, s_tab = sem("pads_made"), sem("pads_sent"), sem("table_steps"), sem("table_made")
        s_got = [sem(f"rows_got{i}") for i in range(U)]
        s_back = [sem(f"results_sent{i}") for i in range(U)]
        s_gTraw, s_gT, s_up, s_gelu = sem("gotT_in_psum"), sem("gotT_made"), sem("hidden_in_psum"), sem("hidden_made")
        s_hTraw, s_hT, s_down, s_y = sem("hiddenT_in_psum"), sem("hiddenT_made"), sem("y_in_psum"), sem("y_weighted")
        s_read = [sem(f"results_read{i}") for i in range(2)]
        s_plain = sem("waits_standing_alone")
        s_sum, s_out = sem("results_added"), sem("out_written")

        block = ctx.enter_context(nc.Block())

        def cv(at, n):
            return consts[:, at:at + n]

        def x_of(n):
            return x[:, bass.ts(n, P)]

        ident = cv(C_IDENT, P)

        def key_step(j):
            first, second = KEYS_OF[j]
            at = BLOCK_ORDER.index(first)
            return at, (NBLK if second is None else BLOCK_ORDER.index(second)) - at

        def pair_of_blocks(tile, j):
            at, step = key_step(j)
            n = tile.ndim if hasattr(tile, "ndim") else 2
            if n == 2:
                v = tile.rearrange("p (b k) -> p b k", k=BLK)
                return v[:, at:at + step + 1:step, :]
            v = tile.rearrange("p h (b k) -> p h b k", k=BLK)
            return v[:, :, at:at + step + 1:step, :]

        FIRST, LOOP_FROM, LOOP_PAIRS = -4, 2, (B - 6) // 2

        def steps(eng, step):
            for c in range(FIRST, LOOP_FROM):
                step(0, c, 0 <= c + 3 < B)
            with eng.Fori(0, LOOP_PAIRS) as h:
                step(h, LOOP_FROM, True)
                step(h, LOOP_FROM + 1, True)
            for c in range(LOOP_FROM + 2 * LOOP_PAIRS, B + 1):
                step(0, c, False)

        def runs(h, c, lead):
            return not isinstance(h, int) or 0 <= c + lead < B

        def wait(eng, s, value):
            if not isinstance(value, int) or value > 0:
                eng.wait_ge(s, value)

        def plain(eng):
            eng.sem_inc(s_plain, 1)

        @block.sync
        def _(sp):
            xv = x_in.rearrange("b s d -> s b d")
            xs = x[:, :].rearrange("p (b d) -> p b d", d=P)
            sp.dma_start(consts[:, :], consts_in).then_inc(s_w, 16)
            sp.dma_start(xs[:, 0:4, :], xv[:, 0:4, :]).then_inc(s_x[0], 16)
            sp.dma_start(wself[:, :], wself_in).then_inc(s_w, 16)
            sp.dma_start(wcross[:, :], wcross_in).then_inc(s_w, 16)
            sp.dma_start(cols[:, :], cols_in).then_inc(s_w, 16)
            sp.dma_start(rows[:, :], rows_in.partition_broadcast(P)).then_inc(s_w, 16)
            sp.dma_start(gate[:, :], gate_in).then_inc(s_w, 16)
            for b in (4, 11, 18, 25):
                sp.dma_start(xs[:, b:b + 7, :], xv[:, b:b + 7, :]).then_inc(s_x[1], 16)
            sp.dma_start(w1[:, :], w1_in).then_inc(s_moe_w, 16)
            sp.dma_start(w2[:, :], w2_in).then_inc(s_moe_w, 16)
            for slot in range(2):
                sp.dma_start(ctxT[:, slot, :], ctxT_in[slot]).then_inc(s_ctx[slot], 16)
            if parts > 1:
              with sp.Fori(1, B // 2) as h:
                for slot in range(2):
                    sp.wait_ge(s_vraw, 2 * h + (B + slot - 1))
                    sp.dma_start(ctxT[:, slot, :], ctxT_in[bass.ds(2 * h + slot, 1)].rearrange("o p t -> (o p) t")).then_inc(s_ctx[slot], 16)
            if parts > 2:
                for slot in range(U):
                    sp.wait_ge(s_back[slot], 16 * BLOCKS // U)
                rv = results.rearrange("(n s) d -> s n d", s=P)
                ov = out.rearrange("b s d -> s b d")

                def read(t):
                    if t >= 2:
                        sp.wait_ge(s_sum, TOPK * (t - 1))
                    for k in range(TOPK):
                        sp.dma_start(back[:, t % 2, k, :, :], rv[:, k * B + t * CH:k * B + (t + 1) * CH, :]).then_inc(s_read[t % 2], 16)
                read(0)
                for t in range(B // CH):
                    if t + 1 < B // CH:
                        read(t + 1)
                    sp.wait_ge(s_sum, TOPK * (t + 1))
                    sp.dma_start(ov[:, t * CH:(t + 1) * CH, :], xs[:, t * CH:(t + 1) * CH, :]).then_inc(s_out, 16)
                sp.wait_ge(s_out, 16 * (B // CH))
            if parts < 3:
                sp.wait_ge(s_res, B * parts)
                sp.dma_start(out.rearrange("b s d -> s b d"), x[:, :].rearrange("p (b d) -> p b d", d=P)).then_inc(s_w, 16)
                sp.wait_ge(s_w, 16 * 7)

        def attention(kind):
            base = B * kind
            own = kind == 0
            w = wself if own else wcross
            wq, wqr, wk, wkr, wv, wo = (
                [w[:, i * P:(i + 1) * P] for i in range(6)] if own
                else [w[:, 0:P], None, w[:, P:2 * P], None, w[:, 2 * P:3 * P], w[:, 3 * P:4 * P]])

            def pe_step(h, c, _):
                def at(lead):
                    return 2 * h + (c + lead)

                def count(lead):
                    return 2 * h + (c + lead + base)
                if runs(h, c, 1):
                    n = count(1)
                    wait(nc.tensor, s_probs, n)
                    for half in range(2):
                        nc.tensor.matmul(p_scores[half][:, :], ident_bf[:, :],
                                         masks_bf[:, kind * WIN:(kind + 1) * WIN].unsqueeze(1).to_broadcast([P, HEADS // 2, WIN]),
                                         start=True, stop=False, skip_group_check=True)
                    nc.tensor.wait_ge(s_spread, n + 1)
                    for r in range(NG):
                        for j in range(NBLK):
                            out_ = p_scores[r // 2][j * BLK:(j + 1) * BLK, (r % 2) * G * WIN:(r % 2 + 1) * G * WIN]
                            mm = nc.tensor.matmul(out_, q_groups[:, r, j * BLK:(j + 1) * BLK],
                                                  pair_of_blocks(k_heads[:, :, :], j),
                                                  start=False, stop=(r % 2 == 1), skip_group_check=True)
                    mm.then_inc(s_scores, 1)
                if runs(h, c, -1):
                    n = count(-1)
                    nc.tensor.wait_ge(s_att, n + 1)
                    wait(nc.tensor, s_aT, n)
                    wait(nc.tensor, s_res, n)
                    if runs(h, c, 2):
                        nc.tensor.wait_ge(s_xT, count(2) + 1)
                    nc.tensor.transpose(p_attT, att[:, :], ident).then_inc(s_aTraw, 1)
                if runs(h, c, 2):
                    n = count(2)
                    nc.tensor.wait_ge(s_xT, n + 1)
                    wait(nc.tensor, s_qk, n)
                    q_tokens = xnT[:, (c + 2) % 2, :].rearrange("p (lo hi k) -> p hi lo k", lo=2, k=BLK)
                    if own:
                        nc.tensor.matmul(p_qk[:, 0:P], wq, q_tokens, start=True, stop=True)
                        nc.tensor.matmul(p_qk[:, P:2 * P], wk, xnT[:, (c + 2) % 2, :], start=True, stop=True)
                        nc.tensor.matmul(p_qk[:, 2 * P:3 * P], wqr, q_tokens, start=True, stop=True)
                        nc.tensor.matmul(p_qk[:, 3 * P:4 * P], wkr, xnT[:, (c + 2) % 2, :], start=True, stop=True).then_inc(s_qkraw, 1)
                    else:
                        slot = (c + 2) % 2
                        nc.tensor.matmul(p_qk[:, 0:P], wq, q_tokens, start=True, stop=True)
                        nc.tensor.wait_ge(s_ctx[slot], 16 * h + 16 * ((c + 2) // 2 + 1))
                        nc.tensor.matmul(p_qk[:, P:2 * P], wk, ctxT[:, slot, :], start=True, stop=True).then_inc(s_qkraw, 1)
                if runs(h, c, -1):
                    n = count(-1)
                    nc.tensor.wait_ge(s_aT, n + 1)
                    nc.tensor.matmul(p_proj, attT[:, :], wo, start=True, stop=True).then_inc(s_proj, 1)
                if runs(h, c, 0):
                    n = count(0)
                    nc.tensor.wait_ge(s_probs, n + 1)
                    wait(nc.tensor, s_pT, n)
                    for m in range(PAIRS):
                        mm = nc.tensor.transpose(p_probsT[m // 4][:, (m % 4) * P:(m % 4 + 1) * P],
                                                 probs[:, m * P:(m + 1) * P], ident)
                    mm.then_inc(s_pTraw, 1)
                if runs(h, c, 1):
                    n = count(1)
                    nc.tensor.wait_ge(s_max, n + 1)
                    for half in range(2):
                        mm = nc.tensor.matmul(p_scores[half][:, :], minus_ident_bf[:, :],
                                              shift[:, half * 8:half * 8 + 8].unsqueeze(2).to_broadcast([P, 8, WIN]),
                                              start=False, stop=True, skip_group_check=True)
                    mm.then_inc(s_shifted, 1)
                if runs(h, c, 3):
                    n = count(3)
                    nc.tensor.wait_ge(s_xn, n + 1)
                    wait(nc.tensor, s_xT, n)
                    wait(nc.tensor, s_res, count(0) if runs(h, c, -1) else 0)
                    nc.tensor.transpose(p_xT, xn[:, :], ident).then_inc(s_xTraw, 1)
                if runs(h, c, 2):
                    n = count(2)
                    wait(nc.tensor, s_v, n)
                    src = xnT[:, (c + 2) % 2, :] if own else ctxT[:, (c + 2) % 2, :]
                    for t, j in enumerate((1, 2, 3)):
                        at0, step = key_step(j)
                        for quarter in range(4):
                            pos = at0 + step * (quarter % 2)
                            mm = nc.tensor.matmul(p_v[quarter * BLK:(quarter + 1) * BLK, t * P:(t + 1) * P],
                                                  src[:, pos * BLK:(pos + 1) * BLK], wv, start=True, stop=True)
                    mm.then_inc(s_vraw, 1)
                if runs(h, c, 0):
                    n = count(0)
                    slot = c % 2
                    nc.tensor.wait_ge(s_pT, n + 1)
                    nc.tensor.wait_ge(s_v, n + 1)
                    wait(nc.tensor, s_att, n)
                    for m in range(PAIRS):
                        for j in range(NBLK):
                            mm = nc.tensor.matmul(p_att[j * BLK:(j + 1) * BLK, m * VC:(m + 1) * VC],
                                                  probsT[:, m, j * BLK:(j + 1) * BLK], values[:, slot, j, m, :],
                                                  start=True, stop=True)
                    mm.then_inc(s_attraw, 1)

            def act_step(h, c, _):
                def count(lead):
                    return 2 * h + (c + lead + base)
                if runs(h, c, -1):
                    n = count(-1)
                    nc.scalar.wait_ge(s_aTraw, n + 1)
                    wait(nc.scalar, s_proj, n)
                    nc.scalar.copy(attT[:, :], p_attT).then_inc(s_aT, 1)
                if runs(h, c, 0):
                    n = count(0)
                    nc.scalar.wait_ge(s_pTraw, n + 1)
                    wait(nc.scalar, s_attraw, n)
                    for half in range(2):
                        a = nc.scalar.copy(probsT[:, 4 * half:4 * half + 4, :],
                                           p_probsT[half][:, :].rearrange("p (m q) -> p m q", q=P))
                    a.then_inc(s_pT, 1)
                if runs(h, c, 1):
                    n = count(1)
                    nc.scalar.wait_ge(s_shifted, n + 1)
                    wait(nc.scalar, s_pTraw, n)
                    for half in range(2):
                        a = nc.scalar.activation(probs[:, half * 512:half * 512 + 512], p_scores[half][:, :], ACT.Exp, scale=SCALE)
                    a.then_inc(s_probs, 1)
                if runs(h, c, 3):
                    n = count(3)
                    nc.scalar.wait_ge(s_xTraw, n + 1)
                    wait(nc.scalar, s_vraw, n - 1)
                    nc.scalar.copy(xnT[:, (c + 3) % 2, :].rearrange("p (lo hi k) -> p lo hi k", lo=2, k=BLK),
                                   p_xT.rearrange("p (hi lo k) -> p lo hi k", lo=2, k=BLK)).then_inc(s_xT, 1)

            def pool_step(h, c, _):
                def count(lead):
                    return 2 * h + (c + lead + base)
                if runs(h, c, 2):
                    n = count(2)
                    nc.gpsimd.wait_ge(s_qk, n + 1)
                    wait(nc.gpsimd, s_scores, n)
                    nc.gpsimd.tensor_tensor(k_heads[:, :, 0:P], qk[:, 1:2, :].to_broadcast([P, G, P]),
                                            cv(C_HEAD, G).unsqueeze(2).to_broadcast([P, G, P]), ALU.mult)
                    nc.gpsimd.tensor_tensor(q_groups[:, :, :], qk[:, 0:1, :].to_broadcast([P, NG, P]),
                                            cv(C_GROUP, NG).unsqueeze(2).to_broadcast([P, NG, P]), ALU.mult).then_inc(s_spread, 1)
                if runs(h, c, 4):
                    pool_rstd(count(4))
                    if not own:
                        nc.gpsimd.wait_ge(s_xn, count(4) + 1)
                        nc.gpsimd.tensor_tensor(x_of(2 * h + (c + 4)), x_of(2 * h + (c + 4)), rows[:, P:2 * P], ALU.add).then_inc(s_bo, 1)

            def dve_step(h, c, _):
                def at(lead):
                    return 2 * h + (c + lead)

                def count(lead):
                    return 2 * h + (c + lead + base)
                if runs(h, c, 1):
                    n = count(1)
                    nc.vector.wait_ge(s_scores, n + 1)
                    wait(nc.vector, s_shifted, n)
                    for half in range(2):
                        a = nc.vector.tensor_reduce(shift[:, half * 8:half * 8 + 8],
                                                    p_scores[half][:, :].rearrange("p (h k) -> p h k", k=WIN), AX.X, ALU.max)
                    a.then_inc(s_max, 1)
                if runs(h, c, -1):
                    n = count(-1)
                    nc.vector.wait_ge(s_proj, n + 1)
                    if not own:
                        nc.vector.wait_ge(s_bo, n - base + 1)
                    nc.vector.tensor_tensor(x_of(at(-1)), x_of(at(-1)), p_proj, ALU.add).then_inc(s_res, 1)
                if runs(h, c, 2):
                    n = count(2)
                    nc.vector.wait_ge(s_qkraw, n + 1)
                    wait(nc.vector, s_spread, n)
                    if own:
                        pq = p_qk[:, :].rearrange("p (t f k) -> p t f k", t=2, f=2)
                        nc.vector.tensor_tensor(turned_cos[:, :, :], pq[:, 0], cv(C_COS, 2 * P).rearrange("p (f k) -> p f k", f=2), ALU.mult)
                        nc.vector.tensor_tensor(turned_sin[:, :, :], pq[:, 1], cv(C_SIN, 2 * P).rearrange("p (f k) -> p f k", f=2), ALU.mult).then_inc(s_rot, 1)
                        nc.vector.wait_ge(s_rot, n + 1)
                        nc.vector.tensor_tensor(qk[:, :, :], turned_cos[:, :, :], turned_sin[:, :, :], ALU.add).then_inc(s_qk, 1)
                    else:
                        nc.vector.tensor_scalar(qk[:, 0, :], p_qk[:, 0:P], cols[:, 0:1], None, ALU.add)
                        nc.vector.tensor_scalar(qk[:, 1, :], p_qk[:, P:2 * P], cols[:, 1:2], None, ALU.add).then_inc(s_qk, 1)
                if runs(h, c, 4):
                    dve_stats(at(4), count(4))
                if runs(h, c, 0):
                    n = count(0)
                    nc.vector.wait_ge(s_attraw, n + 1)
                    pairs = p_att[:, 0:PAIRS * VC].rearrange("p (m v) -> p m v", v=VC)
                    nc.vector.reciprocal(inv_sum[:, :, :], pairs[:, :, 2 * HD:VC]).then_inc(s_inv, 1)
                    nc.vector.wait_ge(s_inv, n + 1)
                    wait(nc.vector, s_aTraw, n)
                    nc.vector.tensor_tensor(att[:, :].rearrange("p (m t d) -> p m t d", t=2, d=HD),
                                            pairs[:, :, 0:2 * HD].rearrange("p m (t d) -> p m t d", t=2),
                                            inv_sum[:, :, :].unsqueeze(3).to_broadcast([P, PAIRS, 2, HD]), ALU.mult).then_inc(s_att, 1)
                if runs(h, c, 2):
                    n = count(2)
                    slot = (c + 2) % 2
                    nc.vector.wait_ge(s_vraw, n + 1)
                    wait(nc.vector, s_attraw, n - 1)
                    if n_is_first(n):
                        nc.vector.wait_ge(s_zero, 3)
                    for t in range(2):
                        lo = t * WIN
                        for j0, j1, n_rows in ((1, NBLK, WIN), (0, 1, BLK)):
                            src_j = 0 if j0 == 0 else j0 - 1
                            src = p_v[lo:lo + n_rows, src_j * P:(src_j + j1 - j0) * P].rearrange(
                                "p (j m t d) -> p j m t d", m=PAIRS, t=2, d=HD)[:, :, :, t, :]
                            dst = values[lo:lo + n_rows, slot, j0:j1, :, t * HD:(t + 1) * HD]
                            if own:
                                a = nc.vector.tensor_copy(dst, src)
                            else:
                                bv = rows[lo:lo + n_rows, 0:P].rearrange("p (m t d) -> p m t d", t=2, d=HD)[:, :, t, :]
                                for j in range(j1 - j0):
                                    a = nc.vector.tensor_tensor(dst[:, j], src[:, j], bv, ALU.add)
                    a.then_inc(s_v, 1)
                if runs(h, c, 4):
                    n = count(4)
                    dve_normalise(at(4), n, xn[:, :])

            return pe_step, act_step, pool_step, dve_step

        def n_is_first(n):
            return isinstance(n, int) and n == 0

        def pool_rstd(n):
            nc.gpsimd.wait_ge(s_mv, n + 1)
            wait(nc.gpsimd, s_xn, n)
            nc.gpsimd.tensor_tensor(var_eps[:, :], mean_var[:, 1:2], eps[:, :], ALU.add).then_inc(s_ve, 1)
            nc.gpsimd.wait_ge(s_ve, n + 1)
            nc.gpsimd.tensor_tensor(rstd[:, :], var_eps[:, :], minus_half[:, :], ALU.pow).then_inc(s_rstd, 1)

        def dve_stats(at, n):
            nc.vector.bn_stats(stats[:, :], x_of(at)).then_inc(s_stats, 1)
            nc.vector.wait_ge(s_stats, n + 1)
            plain(nc.vector)
            nc.vector.bn_aggr(mean_var[:, :], stats[:, :]).then_inc(s_mv, 1)

        def dve_normalise(at, n, dst):
            nc.vector.wait_ge(s_rstd, n + 1)
            nc.vector.wait_ge(s_mv, n + 1)
            wait(nc.vector, s_xTraw, n)
            nc.vector.tensor_scalar(dst, x_of(at), mean_var[:, 0:1], rstd[:, 0:1], ALU.subtract, ALU.mult).then_inc(s_xn, 1)

        ROUTE_STEPS = 14

        def route_steps(eng, step):
            step(0, -1)
            step(0, 0)
            with eng.Fori(0, (B - 2) // 2) as h:
                step(h, 1)
                step(h, 2)
            step(0, B - 1)

        def there(h, c, lead):
            return not isinstance(h, int) or 0 <= c + lead < B

        RBASE = 2 * B

        def route_pe(h, c):
            n = 2 * h + c
            if there(h, c, 0):
                nc.tensor.wait_ge(s_xT, n + (RBASE - B + 1) + B)
                wait(nc.tensor, s_route, ROUTE_STEPS * n - (ROUTE_STEPS - 1))
                nc.tensor.matmul(p_logits, xT_gate[:, :], gate[:, :], start=True, stop=True).then_inc(s_gate, 1)
            if there(h, c, 1):
                m = n + 1 + RBASE
                nc.tensor.wait_ge(s_xn, m + 1)
                wait(nc.tensor, s_xT, m)
                nc.tensor.transpose(p_xT, row[:, (c + 1) % 2, 0, 0:P], ident).then_inc(s_xTraw, 1)
            if there(h, c, 0):
                nc.tensor.wait_ge(s_onehot, n + 1)
                wait(nc.tensor, s_slot, n)
                flat = onehot[:, :, :].rearrange("p k e -> p (k e)")
                nc.tensor.matmul(p_place, cv(C_BEFORE, P), flat, start=True, stop=True)
                nc.tensor.matmul(p_total, ones[:, :], flat, start=True, stop=True).then_inc(s_placed, 1)

        def route_act(h, c):
            n = 2 * h + c
            if there(h, c, 1):
                m = n + 1
                slot = (c + 1) % 2
                nc.scalar.wait_ge(s_xTraw, m + RBASE + 1)
                wait(nc.scalar, s_gate, m)
                nc.scalar.copy(xT_gate[:, :], p_xT).then_inc(s_xT, 1)
                nc.scalar.copy(row[:, slot, 1, 0:P], row[:, slot, 0, 0:P]).then_inc(s_twin, 1)
            if there(h, c, 0):
                nc.scalar.wait_ge(s_route, ROUTE_STEPS * n + 2)
                wait(nc.scalar, s_route, ROUTE_STEPS * n - ROUTE_STEPS + 9)
                nc.scalar.activation(ratio[:, :], top[:, 0:1], ACT.Exp, bias=top[:, 1:2], scale=-1.0).then_inc(s_ratio, 1)

        def route_pool(h, c):
            n = 2 * h + c
            if there(h, c, 1):
                pool_rstd(n + 1 + RBASE)
            if there(h, c, 0):
                slot = c % 2
                nc.gpsimd.wait_ge(s_slot, n + 1)
                nc.gpsimd.wait_ge(s_twin, n + 1)
                plain(nc.gpsimd)
                for k in range(TOPK):
                    nc.gpsimd.indirect_dma_start(out=sent, out_offset=bass.IndirectOffsetOnAxis(ap=slot_u[:, slot, k:k + 1], axis=0),
                                                 in_=row[:, slot, k, :], in_offset=None).then_inc(s_sent[slot], 16)

        def route_dve(h, c):
            n = 2 * h + c
            V = nc.vector
            if there(h, c, 1):
                if not isinstance(h, int) or c + 1 >= 2:
                    V.wait_ge(s_sent[(c + 1) % 2], 32 * h + 32 * ((c + 1) // 2))
                dve_stats(n + 1, n + 1 + RBASE)
                dve_normalise(n + 1, n + 1 + RBASE, row[:, (c + 1) % 2, 0, 0:P])
            if there(h, c, 0):
                slot = c % 2

                def done(op, j):
                    op.then_inc(s_route, 1)

                def needs(j):
                    V.wait_ge(s_route, ROUTE_STEPS * n + j)
                V.wait_ge(s_gate, n + 1)
                done(V.tensor_copy(logits[:, :], p_logits), 1)
                needs(1)
                wait(V, s_ratio, n)
                plain(V)
                done(V.max(top[:, :], logits[:, :]), 2)
                needs(2)
                plain(V)
                done(V.max_index(top_at[:, :], top[:, :], logits[:, :]), 3)
                needs(3)
                done(V.tensor_copy(top_atf[:, :], top_at[:, 0:TOPK]), 4)
                needs(4)
                wait(V, s_placed, n)
                V.tensor_scalar(onehot[:, 0, :], cv(C_IOTA, E), top_atf[:, 0:1], None, ALU.is_equal)
                V.tensor_scalar(onehot[:, 1, :], cv(C_IOTA, E), top_atf[:, 1:2], None, ALU.is_equal).then_inc(s_onehot, 1)
                V.wait_ge(s_ratio, n + 1)
                done(V.tensor_scalar(ratio1[:, :], ratio[:, :], 1.0, None, ALU.add), 5)
                needs(5)
                done(V.reciprocal(row[:, slot, 0, P:P + 1], ratio1[:, :]), 6)
                needs(6)
                done(V.tensor_tensor(row[:, slot, 1, P:P + 1], row[:, slot, 0, P:P + 1], ratio[:, :], ALU.mult), 7)
                done(V.tensor_copy(row[:, slot, :, P + 1:P + 2], result_no[:, :].unsqueeze(2)), 8)
                needs(8)
                done(V.tensor_scalar(result_no[:, :], result_no[:, :], float(P), None, ALU.add), 9)
                V.wait_ge(s_placed, n + 1)
                V.wait_ge(s_onehot, n + 1)
                done(V.tensor_tensor(begin[:, 1, :], begin[:, 0, :], p_total[:, 0:E], ALU.add), 10)
                needs(10)
                done(V.tensor_tensor(place[:, :, :], begin[:, 0:TOPK, :], p_place.rearrange("p (k e) -> p k e", e=E), ALU.add), 11)
                needs(11)
                done(V.tensor_tensor(mine[:, :, :], place[:, :, :], onehot[:, :, :], ALU.mult), 12)
                done(V.tensor_tensor(begin[:, 0, :], begin[:, 1, :], p_total[:, E:2 * E], ALU.add), 13)
                needs(13)
                done(V.tensor_reduce(slot_f[:, :], mine[:, :, :], AX.X, ALU.add), 14)
                needs(14)
                V.tensor_copy(slot_u[:, slot, :], slot_f[:, :]).then_inc(s_slot, 1)

        def route_table():
            V = nc.vector
            count = [0]

            def chain(op):
                op.then_inc(s_table, 1)
                count[0] += 1
                V.wait_ge(s_table, count[0])
            taken = begin[:, 0, :]
            V.wait_ge(s_slot, B)
            chain(V.tensor_scalar(pad_f[:, 0:E], taken, consts[:, C_ROWNO:C_ROWNO + 1], None, ALU.add))
            chain(V.tensor_scalar(pad_f[:, E:E + 1], consts[:, C_ROWNO:C_ROWNO + 1], float(E * CAP), None, ALU.add))
            V.tensor_copy(pad_u[:, :], pad_f[:, :]).then_inc(s_pads, 1)
            chain(V.tensor_tensor(nblocks[:, :], taken, cv(C_REGION, E), ALU.subtract))
            chain(V.tensor_scalar(count_i[:, :], nblocks[:, :], float(P - 1), None, ALU.add))
            chain(V.tensor_scalar(nblocks_i[:, :], count_i[:, :], 7, None, ALU.arith_shift_right))
            chain(V.tensor_copy(ends[:, 0, :], nblocks_i[:, :]))
            for s_, step in enumerate((1, 2, 4)):
                V.tensor_copy(ends[:, s_ + 1, 0:step], ends[:, s_, 0:step])
                chain(V.tensor_tensor(ends[:, s_ + 1, step:E], ends[:, s_, step:E], ends[:, s_, 0:E - step], ALU.add))
            chain(V.tensor_scalar(skip[:, :], ends[:, 0, :], -float(P), float(CAP), ALU.mult, ALU.add))
            number = cv(C_BLOCKNO, BLOCKS)
            chain(V.tensor_tensor(past[:, :, :], number.unsqueeze(2).to_broadcast([P, BLOCKS, E]),
                                  ends[:, 3:4, :].to_broadcast([P, BLOCKS, E]), ALU.is_ge))
            chain(V.tensor_reduce(block_f[:, 0, :], past[:, :, :], AX.X, ALU.add))
            chain(V.tensor_scalar(block_f[:, 0, :], block_f[:, 0, :], float(E - 1), float(F), ALU.min, ALU.mult))
            chain(V.tensor_tensor(past[:, :, :], past[:, :, :], skip[:, :].unsqueeze(1).to_broadcast([P, BLOCKS, E]), ALU.mult))
            chain(V.tensor_reduce(block_f[:, 1, :], past[:, :, :], AX.X, ALU.add))
            chain(V.scalar_tensor_tensor(out=block_f[:, 1, :], in0=number, scalar=float(P), in1=block_f[:, 1, :], op0=ALU.mult, op1=ALU.add))
            chain(V.tensor_scalar(block_f[:, 1, :], block_f[:, 1, :], float(E * CAP), None, ALU.min))
            V.tensor_copy(block_tab[:, :, :], block_f[:, :, :]).then_inc(s_tab, 1)

        LEAD = 4

        def expert_steps(eng, step):
            loop_from = U + 1
            turns = (BLOCKS - LEAD - loop_from) // U
            cols = {}
            for c in range(-2, loop_from):
                step(0, c, cols)
            with eng.Fori(0, turns) as h:
                cols = {}
                for c in range(loop_from, loop_from + U):
                    step(h, c, cols)
            cols = {}
            for c in range(loop_from + U * turns, BLOCKS + 1):
                step(0, c, cols)

        def block_there(h, c, lead):
            return not isinstance(h, int) or 0 <= c + lead < BLOCKS

        def table_at(which, i):
            return block_tab[0:1, which, bass.ds(i, 1)]

        def expert_pe(h, c, cols):
            n = U * h + c

            def col(lead):
                if c + lead not in cols:
                    cols[c + lead] = nc.tensor.value_load(table_at(0, n + lead), min_val=0, max_val=(E - 1) * F)
                return cols[c + lead]
            if block_there(h, c, 0):
                at = col(0)
                nc.tensor.wait_ge(s_gT, n + 1)
                wait(nc.tensor, s_gelu, n)
                nc.tensor.matmul(p_hidden[:, :], gotT[:, :], w1[:, bass.ds(at, F)], start=True, stop=True).then_inc(s_up, 1)
            if block_there(h, c, 1) and (not isinstance(h, int) or c >= 0) and c != 2 * U:
                col(1)
            if block_there(h, c, -1):
                at = col(-1)
                nc.tensor.wait_ge(s_hT, n)
                wait(nc.tensor, s_y, n - 1)
                for f in range(FC):
                    mm = nc.tensor.matmul(p_y, hiddenT[:, f, :], w2[:, bass.ds(at + f * P, P)], start=(f == 0), stop=(f == FC - 1))
                mm.then_inc(s_down, 1)
            if block_there(h, c, 1):
                nc.tensor.wait_ge(s_got[(c + 1) % U], 16 * h + 16 * ((c + 1) // U + 1))
                wait(nc.tensor, s_gT, n + 1)
                nc.tensor.transpose(p_gotT, got[:, (c + 1) % U, 0:P], ident).then_inc(s_gTraw, 1)
            if block_there(h, c, 0):
                nc.tensor.wait_ge(s_gelu, n + 1)
                wait(nc.tensor, s_hT, n)
                for f in range(FC):
                    mm = nc.tensor.transpose(p_hiddenT[:, f * P:(f + 1) * P], hidden[:, f * P:(f + 1) * P], ident)
                mm.then_inc(s_hTraw, 1)

        def read_rows(h, c, lead, n):
            slot = (c + lead) % U
            if not isinstance(h, int) or c + lead >= U:
                nc.scalar.wait_ge(s_y, n + lead + 1 - U)
            first = nc.scalar.value_load(table_at(1, n + lead), min_val=0, max_val=E * CAP)
            nc.scalar.dma_start(got[:, slot, :], sent[bass.ds(first, P), :]).then_inc(s_got[slot], 16)

        def expert_act(h, c, _):
            n = U * h + c
            if isinstance(h, int) and c == -2:
                for lead in range(2, LEAD + 1):
                    read_rows(h, c, lead, n)
            elif block_there(h, c, LEAD):
                read_rows(h, c, LEAD, n)
            if block_there(h, c, 0):
                nc.scalar.wait_ge(s_up, n + 1)
                wait(nc.scalar, s_hTraw, n)
                nc.scalar.activation(hidden[:, :], p_hidden[:, :], ACT.Gelu).then_inc(s_gelu, 1)
            if block_there(h, c, 1):
                nc.scalar.wait_ge(s_gTraw, n + 2)
                wait(nc.scalar, s_up, n + 1)
                nc.scalar.copy(gotT[:, :], p_gotT).then_inc(s_gT, 1)

        def expert_dve(h, c, _):
            n = U * h + c
            if block_there(h, c, -1):
                slot = (c - 1) % U
                nc.vector.wait_ge(s_down, n)
                if not isinstance(h, int) or c - 1 >= U:
                    nc.vector.wait_ge(s_back[slot], 16 * h + 16 * ((c - 1) // U))
                nc.vector.wait_ge(s_got[slot], 16 * h + 16 * ((c - 1) // U + 1))
                nc.vector.tensor_copy(result_at[:, slot:slot + 1], got[:, slot, P + 1:P + 2])
                nc.vector.tensor_scalar(weighted[:, slot, :], p_y, got[:, slot, P:P + 1], None, ALU.mult).then_inc(s_y, 1)
            if block_there(h, c, 0):
                nc.vector.wait_ge(s_hTraw, n + 1)
                wait(nc.vector, s_down, n)
                nc.vector.tensor_copy(hiddenT[:, :, :], p_hiddenT[:, :].rearrange("p (f t) -> p f t", t=P)).then_inc(s_hT, 1)

        def expert_pool(h, c, _):
            n = U * h + c
            if block_there(h, c, -1):
                slot = (c - 1) % U
                nc.gpsimd.wait_ge(s_y, n)
                plain(nc.gpsimd)
                nc.gpsimd.indirect_dma_start(out=results, out_offset=bass.IndirectOffsetOnAxis(ap=result_at[:, slot:slot + 1], axis=0),
                                             in_=weighted[:, slot, :], in_offset=None,
                                             bounds_check=TOPK * TOKENS - 1, oob_is_err=False).then_inc(s_back[slot], 16)

        kinds = [attention(0), attention(1)]

        @block.tensor
        def _(pe):
            pe.wait_ge(s_w, 16 * 6)
            pe.wait_ge(s_const, 6)
            pe.wait_ge(s_zero, 4)
            for k in range(min(parts, 2)):
                steps(pe, kinds[k][0])
            if parts > 2:
                pe.wait_ge(s_res, 2 * B)
                route_steps(pe, route_pe)
                pe.wait_ge(s_slot, B)
                pe.wait_ge(s_moe_w, 32)
                pe.wait_ge(s_tab, 1)
                expert_steps(pe, expert_pe)

        @block.scalar
        def _(act):
            for k in range(min(parts, 2)):
                steps(act, kinds[k][1])
            if parts > 2:
                route_steps(act, route_act)
                act.wait_ge(s_tab, 1)
                for slot in range(2):
                    act.wait_ge(s_sent[slot], 16 * TOPK * B // 2)
                act.wait_ge(s_padsent, 16 * (E + 1))
                expert_steps(act, expert_act)

        @block.gpsimd
        def _(pool):
            nc.gpsimd.memset(k_heads[:, :, :], 0.0).then_inc(s_zero, 1)
            pool.wait_ge(s_w, 16 * 6)
            pool.wait_ge(s_const, 6)
            pool.wait_ge(s_zero, 4)
            for k in range(min(parts, 2)):
                steps(pool, kinds[k][2])
            if parts > 2:
                route_steps(pool, route_pool)
                pool.wait_ge(s_pads, 2)
                for e in range(E + 1):
                    nc.gpsimd.indirect_dma_start(out=sent, out_offset=bass.IndirectOffsetOnAxis(ap=pad_u[:, e:e + 1], axis=0),
                                                 in_=pad_row[:, :], in_offset=None).then_inc(s_padsent, 16)
                expert_steps(pool, expert_pool)

        @block.vector
        def _(dve):
            dve.wait_ge(s_w, 16 * 6)
            nc.vector.tensor_copy(ident_bf[:, :], ident).then_inc(s_const, 1)
            nc.vector.tensor_scalar(minus_ident_bf[:, :], ident, -1.0, None, ALU.mult).then_inc(s_const, 1)
            nc.vector.tensor_copy(masks_bf[:, :], cv(C_MASKS, 2 * WIN)).then_inc(s_const, 1)
            nc.vector.memset(eps[:, :], EPS).then_inc(s_const, 1)
            nc.vector.memset(minus_half[:, :], -0.5).then_inc(s_const, 1)
            nc.vector.memset(ones[:, :], 1.0).then_inc(s_const, 1)
            nc.vector.memset(values[:, :, :, :, :], 0.0).then_inc(s_zero, 1)
            dve.wait_ge(s_zero, 2)
            every = values[:, :, :, :, :].rearrange("p s j m v -> p (s j m) v")
            nc.vector.memset(every[0:WIN, :, 2 * HD:2 * HD + 1], 1.0).then_inc(s_zero, 1)
            nc.vector.memset(every[WIN:P, :, 2 * HD + 1:VC], 1.0).then_inc(s_zero, 1)
            dve.wait_ge(s_x[0], 16)
            dve.wait_ge(s_x[1], 64)
            for k in range(min(parts, 2)):
                steps(dve, kinds[k][3])
            if parts > 2:
                nc.vector.memset(row[:, :, :, P + 2:ROW], 0.0)
                nc.vector.memset(pad_row[:, :], 0.0).then_inc(s_pads, 1)
                nc.vector.tensor_copy(begin[:, 0, :], cv(C_REGION, E)).then_inc(s_const, 1)
                nc.vector.tensor_copy(result_no[:, 0:1], consts[:, C_ROWNO:C_ROWNO + 1]).then_inc(s_const, 1)
                nc.vector.tensor_scalar(result_no[:, 1:2], consts[:, C_ROWNO:C_ROWNO + 1], float(TOKENS), None, ALU.add).then_inc(s_const, 1)
                nc.vector.wait_ge(s_pads, 1)
                nc.vector.tensor_scalar(pad_row[:, P + 1:P + 2], consts[:, C_ROWNO:C_ROWNO + 1], float(TOPK * TOKENS), None, ALU.add).then_inc(s_const, 1)
                dve.wait_ge(s_const, 10)
                dve.wait_ge(s_res, 2 * B)
                route_steps(dve, route_dve)
                route_table()
                expert_steps(dve, expert_dve)
                for t in range(B // CH):
                    dve.wait_ge(s_read[t % 2], 32 * (t // 2 + 1))
                    for k in range(TOPK):
                        part = x[:, t * CH * P:(t + 1) * CH * P].rearrange("p (b d) -> p b d", d=P)
                        if k:
                            dve.wait_ge(s_sum, TOPK * t + k)
                        nc.vector.tensor_tensor(part, part, back[:, t % 2, k, :, :], ALU.add).then_inc(s_sum, 1)


def laid_out(i):
    f = lambda a: np.asarray(a)
    qkv, wo = f(i["L0_attn_w_qkv"]), f(i["L0_attn_w_out"])
    half = np.arange(P).reshape(HEADS, 2, HD // 2)[:, ::-1].reshape(-1)
    q, k, v = qkv[0:P], qkv[P:2 * P], qkv[2 * P:]
    order = np.concatenate([np.arange(b * BLK, (b + 1) * BLK) for b in BLOCK_ORDER])
    c = np.ascontiguousarray
    return {
        "x_in": c(f(i["x"])),
        "ctxT_in": c(f(i["ctx_1024"])[:, order].transpose(0, 2, 1)),
        "consts_in": shape_constants(),
        "wself_in": c(np.concatenate([q.T, q[half].T, k.T, k[half].T, v.T, wo.T], axis=1)),
        "wcross_in": c(np.concatenate([f(i["L0_xattn_W" + s]).T for s in "qkvo"], axis=1)),
        "cols_in": c(np.stack([f(i["L0_xattn_bq"]), f(i["L0_xattn_bk"])], axis=1)),
        "rows_in": c(np.concatenate([f(i["L0_xattn_bv"]), f(i["L0_xattn_bo"])])),
        "gate_in": c(f(i["L0_ffn_gate_w"])),
        "w1_in": c(f(i["L0_ffn_w1"]).transpose(1, 0, 2).reshape(P, E * F)),
        "w2_in": c(f(i["L0_ffn_w2"]).reshape(E, FC, P, P).transpose(2, 0, 1, 3).reshape(P, E * F)),
    }


def kernel(**inputs):
    import concourse.bacc as _bacc
    from concourse.bass_utils import run_bass_kernel_spmd as _run

    nc = _bacc.Bacc("TRN2", target_bir_lowering=False, num_devices=1)
    arrays = laid_out(inputs)
    args = [nc.dram_tensor(n, a.shape, mybir.dt.from_np(a.dtype), kind="ExternalInput").ap() for n, a in arrays.items()]
    out = nc.dram_tensor("out", (B, P, P), mybir.dt.float32, kind="ExternalOutput").ap()
    build(nc, *args, out)
    r = _run(nc, [arrays], core_ids=[0])
    return r.results[0]["out"]
```

```python
import math

import numpy as np

import concourse.bass as bass
from concourse import mybir

P = 128
B = 32
HEADS, HD = 16, 8
BLK = 32
NBLK = P // BLK
G = 4
NG = HEADS // G
WIN = 2 * BLK
PAIRS = HEADS // 2
VC = 2 * HD + 2
SELF_WINDOW, CROSS_WINDOW = 32, 16
SCALE = 1.0 / math.sqrt(HD)
EPS = 1e-5
MASKED = -1e30

E, F, TOPK = 8, 512, 2
FC = F // P
TOKENS = B * P
CAP = TOKENS + P
ROW = P + 4
SLOTS = (TOKENS * TOPK + E * (P - 1)) // P
U = 8
BLOCKS = -(-SLOTS // U) * U

C_IDENT = 0
C_COS = C_IDENT + P
C_SIN = C_COS + 2 * P
C_MASKS = C_SIN + 2 * P
C_HEAD = C_MASKS + 2 * WIN
C_GROUP = C_HEAD + G
C_BEFORE = C_GROUP + NG
C_IOTA = C_BEFORE + P
C_ROWNO = C_IOTA + E
C_REGION = C_ROWNO + 1
C_BLOCKNO = C_REGION + E
C_END = C_BLOCKNO + BLOCKS

KEYS_OF = [(0, None), (0, 1), (2, 1), (2, 3)]
BLOCK_ORDER = (0, 2, 1, 3)


def shape_constants():
    c = np.zeros((P, C_END), np.float32)
    c[:, C_IDENT:C_IDENT + P] = np.eye(P)
    inv = (1.0 / np.float32(10000.0) ** (np.arange(0, HD, 2, dtype=np.float32) / np.float32(HD))).astype(np.float32)
    ang = (np.arange(P, dtype=np.float32)[:, None] * inv[None, :]).astype(np.float32)
    cos, sin = np.cos(ang).astype(np.float32), np.sin(ang).astype(np.float32)
    feat = np.arange(P) % HD
    cosT = cos.T[feat % (HD // 2)]
    sinT = sin.T[feat % (HD // 2)] * np.where(feat < HD // 2, -1.0, 1.0)[:, None]
    order = np.concatenate([np.arange(b * BLK, (b + 1) * BLK) for b in BLOCK_ORDER])
    c[:, C_COS:C_COS + P], c[:, C_COS + P:C_COS + 2 * P] = cosT, cosT[:, order]
    c[:, C_SIN:C_SIN + P], c[:, C_SIN + P:C_SIN + 2 * P] = sinT, sinT[:, order]
    for q in range(P):
        for slot in range(2):
            block = KEYS_OF[q // BLK][slot]
            for k in range(BLK):
                if block is None:
                    own, cross = False, k < min(q + 1, CROSS_WINDOW - 1 - q)
                else:
                    key = block * BLK + k
                    own = key <= q and q - key < SELF_WINDOW
                    cross = key <= q and q - key < CROSS_WINDOW and key - (q - CROSS_WINDOW + 1) <= q
                for n, allowed in enumerate((own, cross)):
                    c[q, C_MASKS + n * WIN + slot * BLK + k] = 0.0 if allowed else MASKED
    for p in range(P):
        c[p, C_HEAD + (p // HD) % G] = 1.0
        c[p, C_GROUP + p // (G * HD)] = 1.0
        c[p, C_BEFORE + p + 1:C_BEFORE + P] = 1.0
        c[p, C_IOTA:C_IOTA + E] = np.arange(E)
        c[p, C_ROWNO] = p
        c[p, C_REGION:C_REGION + E] = np.arange(E) * CAP
        c[p, C_BLOCKNO:C_BLOCKNO + BLOCKS] = np.arange(BLOCKS)
    return c


def build(nc, x_in, ctxT_in, consts_in, wself_in, wcross_in, cols_in, rows_in, gate_in, w1_in, w2_in, out, parts=3):
    from contextlib import ExitStack
    F32, BF16, I32, U32 = mybir.dt.float32, mybir.dt.bfloat16, mybir.dt.int32, mybir.dt.uint32
    ALU, ACT, AX = mybir.AluOpType, mybir.ActivationFunctionType, mybir.AxisListType

    ctx = ExitStack()
    with ctx:
        def sb(name, shape, dt=F32):
            return ctx.enter_context(nc.sbuf_tensor(name, shape, dt))

        def pb(name):
            return ctx.enter_context(nc.psum_tensor(name, [P, 512], F32))

        def sem(name):
            return ctx.enter_context(nc.semaphore(name))

        sent = nc.dram_tensor("sent_rows", [(E + 1) * CAP, ROW], F32, kind="Internal").ap()
        results = nc.dram_tensor("expert_results", [TOPK * TOKENS, P], F32, kind="Internal").ap()

        x = sb("x", [P, B * P])
        consts = sb("consts", [P, C_END])
        wself = sb("wself", [P, 6 * P])
        wcross = sb("wcross", [P, 4 * P])
        cols = sb("cols", [P, 2])
        rows = sb("rows", [P, 2 * P])
        gate = sb("gate", [P, E])
        w1 = sb("w1", [P, E * F])
        w2 = sb("w2", [P, E * F])
        ident_bf = sb("ident_bf", [P, P], BF16)
        minus_ident_bf = sb("minus_ident_bf", [P, P], BF16)
        masks_bf = sb("masks_bf", [P, 2 * WIN], BF16)
        ones_bf = sb("ones_bf", [P, P], BF16)
        before_bf = sb("before_bf", [P, P], BF16)

        stats = sb("stats", [P, 2, 6])
        mean_var = sb("mean_var", [P, 2, 2])
        eps = sb("eps", [P, 1])
        minus_half = sb("minus_half", [P, 1])
        var_eps = sb("var_eps", [P, 2])
        rstd = sb("rstd", [P, 2])
        xn = sb("xn", [P, 2, P])
        xnT = sb("xnT", [P, 2, P])
        ctxT = sb("ctxT", [P, 2, P])
        turned_cos = sb("turned_cos", [P, 2, P])
        turned_sin = sb("turned_sin", [P, 2, P])
        qk = sb("qk", [P, 2, P])
        q_groups = sb("q_groups", [P, NG, P])
        k_heads = sb("k_heads", [P, G, P + BLK])
        shift = sb("shift", [P, HEADS], BF16)
        probs = sb("probs", [P, HEADS * WIN])
        probsT = sb("probsT", [P, PAIRS, P])
        values = sb("values", [P, 4, NBLK, PAIRS, VC])
        inv_sum = sb("inv_sum", [P, PAIRS, 2])
        att = sb("att", [P, P])
        attT = sb("attT", [P, P])

        p_scores = [pb("p_scores0"), pb("p_scores1")]
        p_probsT = [pb("p_probsT0"), pb("p_probsT1")]
        p_qk, p_v, p_att, p_misc = pb("p_qk"), pb("p_v"), pb("p_att"), pb("p_misc")
        p_xT, p_attT, p_proj = p_misc[:, 0:P], p_misc[:, P:2 * P], p_misc[:, 2 * P:3 * P]

        row = sb("row", [P, 4, TOPK, ROW])
        xn3 = sb("xn3", [P, 4, P])
        x3T = sb("x3T", [P, P])
        logits = sb("logits", [P, 2, E])
        top = sb("top", [P, 2, 8])
        top_at = sb("top_at", [P, 2, 8], U32)
        top_atf = sb("top_atf", [P, 2, TOPK])
        ratio = sb("ratio", [P, 2, 1])
        ratio1 = sb("ratio1", [P, 2, 1])
        onehot = sb("onehot", [P, 2 * TOPK + 1, E], BF16)
        begin = sb("begin", [P, E])
        place = sb("place", [P, 2 * TOPK, E])
        mine = sb("mine", [P, 2 * TOPK, E])
        slot_f = sb("slot_f", [P, 2 * TOPK])
        slot_u = sb("slot_u", [P, 4, TOPK], U32)
        result_no = sb("result_no", [P, 2, TOPK])
        pad_row = sb("pad_row", [P, ROW])
        pad_f = sb("pad_f", [P, E + 1])
        pad_u = sb("pad_u", [P, E + 1], U32)
        count_i = sb("count_i", [P, E], I32)
        nblocks_i = sb("nblocks_i", [P, E], I32)
        nblocks = sb("nblocks", [P, E])
        ends = sb("ends", [P, 4, E])
        skip = sb("skip", [P, E])
        past = sb("past", [P, BLOCKS, E])
        block_f = sb("block_f", [P, 2, BLOCKS])
        block_tab = sb("block_tab", [P, 2, BLOCKS], I32)
        p_x3T = p_qk[:, 3 * P:4 * P]
        p_logits, p_place, p_total = p_att[:, 160:160 + 2 * E], p_att[:, 192:192 + (2 * TOPK + 1) * E], p_att[:, 192 + 2 * TOPK * E:192 + (2 * TOPK + 1) * E]

        got = sb("got", [P, U, ROW])
        gotT = sb("gotT", [P, P])
        hidden = sb("hidden", [P, F])
        hiddenT = sb("hiddenT", [P, FC, P])
        weighted = sb("weighted", [P, U, P])
        result_at = sb("result_at", [P, U], U32)
        p_gotT, p_hidden, p_hiddenT, p_y = p_misc[:, 0:P], p_scores[0], p_probsT[0], p_att[:, 0:P]

        CH = 4
        back = sb("back", [P, 2, TOPK, CH, P])

        s_x = [sem(f"x_loaded{i}") for i in range(2)]
        s_w = sem("weights_loaded")
        s_moe_w = sem("expert_weights_loaded")
        s_const = sem("constants_made")
        s_zero = sem("buffers_cleared")
        s_ctx = [sem(f"ctx_loaded{i}") for i in range(2)]
        s_stats, s_mv, s_ve, s_rstd = sem("stats_made"), sem("mean_var_made"), sem("var_eps_made"), sem("rstd_made")
        s_xn, s_xTraw, s_xT = sem("xn_made"), sem("xT_in_psum"), sem("xT_made")
        s_bo = sem("bo_added")
        s_qkraw, s_rot, s_qk = sem("qk_in_psum"), sem("rotary_parts"), sem("qk_made")
        s_spread = sem("qk_spread")
        s_scores, s_max, s_shifted = sem("scores_made"), sem("max_made"), sem("scores_shifted")
        s_probs, s_pTraw, s_pT = sem("probs_made"), sem("probsT_in_psum"), sem("probsT_made")
        s_vraw, s_v = sem("v_in_psum"), sem("v_made")
        s_attraw, s_inv, s_att = sem("att_in_psum"), sem("sums_inverted"), sem("att_made")
        s_aTraw, s_aT, s_proj, s_res = sem("attT_in_psum"), sem("attT_made"), sem("proj_in_psum"), sem("x_updated")

        s_st3, s_xn3, s_x3Traw, s_x3T = sem("stats3_made"), sem("xn3_made"), sem("x3T_in_psum"), sem("x3T_made")
        s_rows, s_gate, s_ratio = sem("rows_filled"), sem("gate_in_psum"), sem("ratio_made")
        s_choose, s_onehot, s_placed = sem("choosing_steps"), sem("onehot_made"), sem("places_in_psum")
        s_place, s_slot, s_begun = sem("placing_steps"), sem("slots_made"), sem("begin_moved")
        s_sent = [sem(f"rows_sent{i}") for i in range(4)]
        s_pads, s_padsent, s_table, s_tab = sem("pads_made"), sem("pads_sent"), sem("table_steps"), sem("table_made")
        s_got = [sem(f"rows_got{i}") for i in range(U)]
        s_back = [sem(f"results_sent{i}") for i in range(U)]
        s_gTraw, s_gT, s_up, s_gelu = sem("gotT_in_psum"), sem("gotT_made"), sem("hidden_in_psum"), sem("hidden_made")
        s_hTraw, s_hT, s_down, s_y = sem("hiddenT_in_psum"), sem("hiddenT_made"), sem("y_in_psum"), sem("y_weighted")
        s_read = [sem(f"results_read{i}") for i in range(2)]
        s_plain = sem("waits_standing_alone")
        s_sum, s_out = sem("results_added"), sem("out_written")

        block = ctx.enter_context(nc.Block())

        def cv(at, n):
            return consts[:, at:at + n]

        def x_of(n):
            return x[:, bass.ts(n, P)]

        ident = cv(C_IDENT, P)

        def key_step(j):
            first, second = KEYS_OF[j]
            at = BLOCK_ORDER.index(first)
            return at, (NBLK if second is None else BLOCK_ORDER.index(second)) - at

        def pair_of_blocks(tile, j):
            at, step = key_step(j)
            n = tile.ndim if hasattr(tile, "ndim") else 2
            if n == 2:
                v = tile.rearrange("p (b k) -> p b k", k=BLK)
                return v[:, at:at + step + 1:step, :]
            v = tile.rearrange("p h (b k) -> p h b k", k=BLK)
            return v[:, :, at:at + step + 1:step, :]

        FIRST = -5
        TURN = 4
        SPAN = [(2, B), (8, B + 5)]

        def steps(eng, kind, step):
            loop_from, last = SPAN[kind]
            turns = (B - 5 - loop_from) // TURN
            for c in range(FIRST, loop_from):
                step(0, c)
            with eng.Fori(0, turns) as h:
                for c in range(loop_from, loop_from + TURN):
                    step(h, c)
            for c in range(loop_from + TURN * turns, last + 1):
                step(0, c)

        def runs(h, c, lead):
            return not isinstance(h, int) or 0 <= c + lead < B

        def wait(eng, s, value):
            if not isinstance(value, int) or value > 0:
                eng.wait_ge(s, value)

        def plain(eng):
            eng.sem_inc(s_plain, 1)

        @block.sync
        def _(sp):
            xv = x_in.rearrange("b s d -> s b d")
            xs = x[:, :].rearrange("p (b d) -> p b d", d=P)
            sp.dma_start(consts[:, :], consts_in).then_inc(s_w, 16)
            sp.dma_start(xs[:, 0:4, :], xv[:, 0:4, :]).then_inc(s_x[0], 16)
            sp.dma_start(wself[:, :], wself_in).then_inc(s_w, 16)
            sp.dma_start(wcross[:, :], wcross_in).then_inc(s_w, 16)
            sp.dma_start(cols[:, :], cols_in).then_inc(s_w, 16)
            sp.dma_start(rows[:, :], rows_in.partition_broadcast(P)).then_inc(s_w, 16)
            sp.dma_start(gate[:, :], gate_in).then_inc(s_w, 16)
            for b in (4, 11, 18, 25):
                sp.dma_start(xs[:, b:b + 7, :], xv[:, b:b + 7, :]).then_inc(s_x[1], 16)
            sp.dma_start(w1[:, :], w1_in).then_inc(s_moe_w, 16)
            sp.dma_start(w2[:, :], w2_in).then_inc(s_moe_w, 16)
            for slot in range(2):
                sp.dma_start(ctxT[:, slot, :], ctxT_in[slot]).then_inc(s_ctx[slot], 16)
            if parts > 1:
              with sp.Fori(1, B // 2) as h:
                for slot in range(2):
                    sp.wait_ge(s_vraw, 2 * h + (B + slot - 1))
                    sp.dma_start(ctxT[:, slot, :], ctxT_in[bass.ds(2 * h + slot, 1)].rearrange("o p t -> (o p) t")).then_inc(s_ctx[slot], 16)
            if parts > 2:
                for slot in range(U):
                    sp.wait_ge(s_back[slot], 16 * BLOCKS // U)
                rv = results.rearrange("(n s) d -> s n d", s=P)
                ov = out.rearrange("b s d -> s b d")

                def read(t):
                    if t >= 2:
                        sp.wait_ge(s_sum, TOPK * (t - 1))
                    for k in range(TOPK):
                        sp.dma_start(back[:, t % 2, k, :, :], rv[:, k * B + t * CH:k * B + (t + 1) * CH, :]).then_inc(s_read[t % 2], 16)
                read(0)
                for t in range(B // CH):
                    if t + 1 < B // CH:
                        read(t + 1)
                    sp.wait_ge(s_sum, TOPK * (t + 1))
                    sp.dma_start(ov[:, t * CH:(t + 1) * CH, :], xs[:, t * CH:(t + 1) * CH, :]).then_inc(s_out, 16)
                sp.wait_ge(s_out, 16 * (B // CH))
            if parts < 3:
                sp.wait_ge(s_res, B * parts)
                sp.dma_start(out.rearrange("b s d -> s b d"), x[:, :].rearrange("p (b d) -> p b d", d=P)).then_inc(s_w, 16)
                sp.wait_ge(s_w, 16 * 7)

        def attention(kind):
            base = B * kind
            own = kind == 0
            w = wself if own else wcross
            wq, wqr, wk, wkr, wv, wo = (
                [w[:, i * P:(i + 1) * P] for i in range(6)] if own
                else [w[:, 0:P], None, w[:, P:2 * P], None, w[:, 2 * P:3 * P], w[:, 3 * P:4 * P]])

            def pe_step(h, c):
                def at(lead):
                    return TURN * h + (c + lead)

                def count(lead):
                    return TURN * h + (c + lead + base)
                if runs(h, c, 1):
                    n = count(1)
                    for half in range(2):
                        wait(nc.tensor, s_probs, 2 * n - 1 + half)
                        nc.tensor.matmul(p_scores[half][:, :], ident_bf[:, :],
                                         masks_bf[:, kind * WIN:(kind + 1) * WIN].unsqueeze(1).to_broadcast([P, HEADS // 2, WIN]),
                                         start=True, stop=False, skip_group_check=True)
                    nc.tensor.wait_ge(s_spread, n + 1)
                    for r in range(NG):
                        for j in range(NBLK):
                            out_ = p_scores[r // 2][j * BLK:(j + 1) * BLK, (r % 2) * G * WIN:(r % 2 + 1) * G * WIN]
                            mm = nc.tensor.matmul(out_, q_groups[:, r, j * BLK:(j + 1) * BLK],
                                                  pair_of_blocks(k_heads[:, :, :], j),
                                                  start=False, stop=(r % 2 == 1), skip_group_check=True)
                        if r % 2 == 1:
                            mm.then_inc(s_scores, 1)
                if runs(h, c, -1):
                    n = count(-1)
                    nc.tensor.wait_ge(s_att, n + 1)
                    wait(nc.tensor, s_aT, n)
                    wait(nc.tensor, s_res, n)
                    if runs(h, c, 2):
                        nc.tensor.wait_ge(s_xT, count(2) + 1)
                    nc.tensor.transpose(p_attT, att[:, :], ident).then_inc(s_aTraw, 1)
                if runs(h, c, 2):
                    n = count(2)
                    nc.tensor.wait_ge(s_xT, n + 1)
                    wait(nc.tensor, s_qk, n)
                    if not own and runs(h, c, -3):
                        nc.tensor.wait_ge(s_x3T, at(-3) + 1)
                    q_tokens = xnT[:, (c + 2) % 2, :].rearrange("p (lo hi k) -> p hi lo k", lo=2, k=BLK)
                    if own:
                        nc.tensor.matmul(p_qk[:, 0:P], wq, q_tokens, start=True, stop=True)
                        nc.tensor.matmul(p_qk[:, P:2 * P], wk, xnT[:, (c + 2) % 2, :], start=True, stop=True)
                        nc.tensor.matmul(p_qk[:, 2 * P:3 * P], wqr, q_tokens, start=True, stop=True)
                        nc.tensor.matmul(p_qk[:, 3 * P:4 * P], wkr, xnT[:, (c + 2) % 2, :], start=True, stop=True).then_inc(s_qkraw, 1)
                    else:
                        slot = (c + 2) % 2
                        nc.tensor.matmul(p_qk[:, 0:P], wq, q_tokens, start=True, stop=True)
                        nc.tensor.wait_ge(s_ctx[slot], 8 * TURN * h + 16 * ((c + 2) // 2 + 1))
                        nc.tensor.matmul(p_qk[:, P:2 * P], wk, ctxT[:, slot, :], start=True, stop=True).then_inc(s_qkraw, 1)
                if runs(h, c, -1):
                    n = count(-1)
                    nc.tensor.wait_ge(s_aT, n + 1)
                    nc.tensor.matmul(p_proj, attT[:, :], wo, start=True, stop=True).then_inc(s_proj, 1)
                if not own:
                    route_pe(h, c)
                if runs(h, c, 0):
                    n = count(0)
                    for m in range(PAIRS):
                        if m % 4 == 0:
                            nc.tensor.wait_ge(s_probs, 2 * n + 1 + m // 4)
                            wait(nc.tensor, s_pT, 2 * n - 1 + m // 4)
                        mm = nc.tensor.transpose(p_probsT[m // 4][:, (m % 4) * P:(m % 4 + 1) * P],
                                                 probs[:, m * P:(m + 1) * P], ident)
                        if m % 4 == 3:
                            mm.then_inc(s_pTraw, 1)
                if runs(h, c, 2):
                    n = count(2)
                    wait(nc.tensor, s_v, n)
                    src = xnT[:, (c + 2) % 2, :] if own else ctxT[:, (c + 2) % 2, :]
                    for t, j in enumerate((1, 2, 3)):
                        at0, step = key_step(j)
                        for quarter in range(4):
                            pos = at0 + step * (quarter % 2)
                            mm = nc.tensor.matmul(p_v[quarter * BLK:(quarter + 1) * BLK, t * P:(t + 1) * P],
                                                  src[:, pos * BLK:(pos + 1) * BLK], wv, start=True, stop=True)
                    mm.then_inc(s_vraw, 1)
                if runs(h, c, 1):
                    n = count(1)
                    for half in range(2):
                        nc.tensor.wait_ge(s_max, 2 * n + 1 + half)
                        mm = nc.tensor.matmul(p_scores[half][:, :], minus_ident_bf[:, :],
                                              shift[:, half * 8:half * 8 + 8].unsqueeze(2).to_broadcast([P, 8, WIN]),
                                              start=False, stop=True, skip_group_check=True)
                        mm.then_inc(s_shifted, 1)
                if runs(h, c, 3):
                    n = count(3)
                    nc.tensor.wait_ge(s_xn, n + 1)
                    wait(nc.tensor, s_xT, n)
                    wait(nc.tensor, s_res, count(0) if runs(h, c, -1) else 0)
                    nc.tensor.transpose(p_xT, xn[:, (c + 3) % 2, :], ident).then_inc(s_xTraw, 1)
                if not own and runs(h, c, -2):
                    n = at(-2)
                    nc.tensor.wait_ge(s_xn3, n + 1)
                    wait(nc.tensor, s_x3T, n)
                    if runs(h, c, 2):
                        nc.tensor.wait_ge(s_qk, count(2) + 1)
                    nc.tensor.transpose(p_x3T, xn3[:, (c - 2) % 4, :], ident).then_inc(s_x3Traw, 1)
                if runs(h, c, 0):
                    n = count(0)
                    slot = c % 4
                    nc.tensor.wait_ge(s_v, n + 1)
                    wait(nc.tensor, s_att, n)
                    if not own:
                        route_bank(nc.tensor, h, c)
                    for m in range(PAIRS):
                        if m % 4 == 0:
                            nc.tensor.wait_ge(s_pT, 2 * n + 1 + m // 4)
                        for j in range(NBLK):
                            mm = nc.tensor.matmul(p_att[j * BLK:(j + 1) * BLK, m * VC:(m + 1) * VC],
                                                  probsT[:, m, j * BLK:(j + 1) * BLK], values[:, slot, j, m, :],
                                                  start=True, stop=True)
                    mm.then_inc(s_attraw, 1)

            def act_step(h, c):
                def count(lead):
                    return TURN * h + (c + lead + base)
                if runs(h, c, -1):
                    n = count(-1)
                    nc.scalar.wait_ge(s_aTraw, n + 1)
                    wait(nc.scalar, s_proj, n)
                    nc.scalar.copy(attT[:, :], p_attT).then_inc(s_aT, 1)
                if not own and runs(h, c, 2):
                    n = count(2)
                    nc.scalar.wait_ge(s_qkraw, n + 1)
                    wait(nc.scalar, s_spread, n)
                    nc.scalar.activation(qk[:, 1, :], p_qk[:, P:2 * P], ACT.Identity, bias=cols[:, 1:2])
                    nc.scalar.activation(qk[:, 0, :], p_qk[:, 0:P], ACT.Identity, bias=cols[:, 0:1]).then_inc(s_qk, 1)
                if runs(h, c, 0):
                    n = count(0)
                    wait(nc.scalar, s_attraw, n)
                    for half in range(2):
                        nc.scalar.wait_ge(s_pTraw, 2 * n + 1 + half)
                        nc.scalar.copy(probsT[:, 4 * half:4 * half + 4, :],
                                       p_probsT[half][:, :].rearrange("p (m q) -> p m q", q=P)).then_inc(s_pT, 1)
                if runs(h, c, 1):
                    n = count(1)
                    for half in range(2):
                        nc.scalar.wait_ge(s_shifted, 2 * n + 1 + half)
                        wait(nc.scalar, s_pTraw, 2 * n - 1 + half)
                        nc.scalar.activation(probs[:, half * 512:half * 512 + 512], p_scores[half][:, :], ACT.Exp, scale=SCALE).then_inc(s_probs, 1)
                if runs(h, c, 3):
                    n = count(3)
                    nc.scalar.wait_ge(s_xTraw, n + 1)
                    wait(nc.scalar, s_vraw, n - 1)
                    nc.scalar.copy(xnT[:, (c + 3) % 2, :].rearrange("p (lo hi k) -> p lo hi k", lo=2, k=BLK),
                                   p_xT.rearrange("p (hi lo k) -> p lo hi k", lo=2, k=BLK)).then_inc(s_xT, 1)
                if not own:
                    fill_rows(h, c)
                    route_act(h, c)
                    ratio_act(h, c)

            def pool_step(h, c):
                def count(lead):
                    return TURN * h + (c + lead + base)
                if runs(h, c, 2):
                    n = count(2)
                    nc.gpsimd.wait_ge(s_qk, n + 1)
                    wait(nc.gpsimd, s_scores, 2 * n)
                    nc.gpsimd.tensor_tensor(k_heads[:, :, 0:P], qk[:, 1:2, :].to_broadcast([P, G, P]),
                                            cv(C_HEAD, G).unsqueeze(2).to_broadcast([P, G, P]), ALU.mult)
                    nc.gpsimd.tensor_tensor(q_groups[:, :, :], qk[:, 0:1, :].to_broadcast([P, NG, P]),
                                            cv(C_GROUP, NG).unsqueeze(2).to_broadcast([P, NG, P]), ALU.mult).then_inc(s_spread, 1)
                if not own:
                    route_pool(h, c)
                if not own and runs(h, c, 4):
                    nc.gpsimd.wait_ge(s_xn, count(4) + 1)
                    nc.gpsimd.tensor_tensor(x_of(TURN * h + (c + 4)), x_of(TURN * h + (c + 4)), rows[:, P:2 * P], ALU.add).then_inc(s_bo, 1)
                if runs(h, c, 5) or (not own and runs(h, c, -1)):
                    n = count(5)
                    both = 1 if own else 2
                    nc.gpsimd.wait_ge(s_mv, n + 1)
                    if runs(h, c, 4):
                        wait(nc.gpsimd, s_xn, n)
                    if not own and runs(h, c, -2):
                        nc.gpsimd.wait_ge(s_xn3, TURN * h + (c - 1))
                    nc.gpsimd.tensor_tensor(var_eps[:, 0:both], mean_var[:, 0:both, 1:2].squeeze(2),
                                            eps[:, 0:1].to_broadcast([P, both]), ALU.add).then_inc(s_ve, 1)
                    nc.gpsimd.wait_ge(s_ve, n + 1)
                    nc.gpsimd.tensor_tensor(rstd[:, 0:both], var_eps[:, 0:both], minus_half[:, 0:1].to_broadcast([P, both]), ALU.pow).then_inc(s_rstd, 1)

            def dve_step(h, c):
                def at(lead):
                    return TURN * h + (c + lead)

                def count(lead):
                    return TURN * h + (c + lead + base)
                norm_now, norm3_now = runs(h, c, 4), not own and runs(h, c, -2)
                if runs(h, c, 1):
                    n = count(1)
                    for half in range(2):
                        nc.vector.wait_ge(s_scores, 2 * n + 1 + half)
                        wait(nc.vector, s_shifted, 2 * n - 1 + half)
                        nc.vector.tensor_reduce(shift[:, half * 8:half * 8 + 8],
                                                    p_scores[half][:, :].rearrange("p (h k) -> p h k", k=WIN), AX.X, ALU.max).then_inc(s_max, 1)
                if runs(h, c, -1):
                    n = count(-1)
                    nc.vector.wait_ge(s_proj, n + 1)
                    if not own:
                        nc.vector.wait_ge(s_bo, n - base + 1)
                    nc.vector.tensor_tensor(x_of(at(-1)), x_of(at(-1)), p_proj, ALU.add).then_inc(s_res, 1)
                if own and runs(h, c, 2):
                    n = count(2)
                    nc.vector.wait_ge(s_qkraw, n + 1)
                    wait(nc.vector, s_spread, n)
                    if True:
                        pq = p_qk[:, :].rearrange("p (t f k) -> p t f k", t=2, f=2)
                        nc.vector.tensor_tensor(turned_cos[:, :, :], pq[:, 0], cv(C_COS, 2 * P).rearrange("p (f k) -> p f k", f=2), ALU.mult)
                        nc.vector.tensor_tensor(turned_sin[:, :, :], pq[:, 1], cv(C_SIN, 2 * P).rearrange("p (f k) -> p f k", f=2), ALU.mult).then_inc(s_rot, 1)
                        nc.vector.wait_ge(s_rot, n + 1)
                        nc.vector.tensor_tensor(qk[:, :, :], turned_cos[:, :, :], turned_sin[:, :, :], ALU.add).then_inc(s_qk, 1)
                if norm_now or norm3_now:
                    n = count(4)
                    nc.vector.wait_ge(s_rstd, n + 1)
                    nc.vector.wait_ge(s_mv, n + 1)
                    if norm_now:
                        wait(nc.vector, s_xTraw, n - 1)
                        a = nc.vector.tensor_scalar(xn[:, c % 2, :], x_of(at(4)), mean_var[:, 0, 0:1], rstd[:, 0:1],
                                                    ALU.subtract, ALU.mult).then_inc(s_xn, 1)
                    if norm3_now:
                        wait(nc.vector, s_rows, at(-2) - 3)
                        a = nc.vector.tensor_scalar(xn3[:, (c - 2) % 4, :], x_of(at(-2)), mean_var[:, 1, 0:1], rstd[:, 1:2],
                                                    ALU.subtract, ALU.mult).then_inc(s_xn3, 1)
                if not own:
                    route_dve_bank(h, c)
                if runs(h, c, 2):
                    n = count(2)
                    slot = (c + 2) % 4
                    nc.vector.wait_ge(s_vraw, n + 1)
                    wait(nc.vector, s_attraw, n - 3)
                    if n_is_first(n):
                        nc.vector.wait_ge(s_zero, 3)
                    for t in range(2):
                        lo = t * WIN
                        for j0, j1, n_rows in ((1, NBLK, WIN), (0, 1, BLK)):
                            src_j = 0 if j0 == 0 else j0 - 1
                            src = p_v[lo:lo + n_rows, src_j * P:(src_j + j1 - j0) * P].rearrange(
                                "p (j m t d) -> p j m t d", m=PAIRS, t=2, d=HD)[:, :, :, t, :]
                            dst = values[lo:lo + n_rows, slot, j0:j1, :, t * HD:(t + 1) * HD]
                            if own:
                                a = nc.vector.tensor_copy(dst, src)
                            else:
                                bv = rows[lo:lo + n_rows, 0:P].rearrange("p (m t d) -> p m t d", t=2, d=HD)[:, :, t, :]
                                a = nc.vector.tensor_tensor(dst, src, bv.unsqueeze(1).to_broadcast([n_rows, j1 - j0, PAIRS, HD]), ALU.add)
                    a.then_inc(s_v, 1)
                if runs(h, c, 0):
                    n = count(0)
                    nc.vector.wait_ge(s_attraw, n + 1)
                    pairs = p_att[:, 0:PAIRS * VC].rearrange("p (m v) -> p m v", v=VC)
                    nc.vector.reciprocal(inv_sum[:, :, :], pairs[:, :, 2 * HD:VC]).then_inc(s_inv, 1)
                    nc.vector.wait_ge(s_inv, n + 1)
                    wait(nc.vector, s_aTraw, n)
                    nc.vector.tensor_tensor(att[:, :].rearrange("p (m t d) -> p m t d", t=2, d=HD),
                                            pairs[:, :, 0:2 * HD].rearrange("p m (t d) -> p m t d", t=2),
                                            inv_sum[:, :, :].unsqueeze(3).to_broadcast([P, PAIRS, 2, HD]), ALU.mult).then_inc(s_att, 1)
                if runs(h, c, 5) or (not own and runs(h, c, -1)):
                    n = count(5)
                    wait(nc.vector, s_rstd, n)
                    if runs(h, c, 5):
                        plain(nc.vector)
                        nc.vector.bn_stats(stats[:, 0, :], x_of(at(5))).then_inc(s_stats, 1)
                    if not own and runs(h, c, -1):
                        nc.vector.wait_ge(s_res, count(-1) + 1)
                        plain(nc.vector)
                        nc.vector.bn_stats(stats[:, 1, :], x_of(at(-1))).then_inc(s_st3, 1)
                    if runs(h, c, 5):
                        nc.vector.wait_ge(s_stats, n + 1)
                        plain(nc.vector)
                        a = nc.vector.bn_aggr(mean_var[:, 0, :], stats[:, 0, :])
                    if not own and runs(h, c, -1):
                        nc.vector.wait_ge(s_st3, at(-1) + 1)
                        plain(nc.vector)
                        a = nc.vector.bn_aggr(mean_var[:, 1, :], stats[:, 1, :])
                    a.then_inc(s_mv, 1)
                if not own:
                    route_dve(h, c)

            return pe_step, act_step, pool_step, dve_step

        def n_is_first(n):
            return isinstance(n, int) and n == 0

        CHOOSE_STEPS, PLACE_STEPS = 6, 8

        def choosing(h, c):
            if c % 2 == 0 and runs(h, c, -4):
                return True, TURN // 2 * h + (c - 4) // 2
            return False, None

        def placing(h, c):
            if c % 2 == 1 and runs(h, c, -5):
                return True, TURN // 2 * h + (c - 5) // 2
            return False, None

        def route_pe(h, c):
            n = TURN * h + (c - 3)
            if runs(h, c, -3):
                nc.tensor.wait_ge(s_x3T, n + 1)
                if c % 2 == 0:
                    wait(nc.tensor, s_begun, TURN // 2 * h + (c - 4) // 2)
                else:
                    wait(nc.tensor, s_choose, CHOOSE_STEPS * (TURN // 2 * h + (c - 5) // 2) + 1)
                t = (c - 3) % 2
                nc.tensor.matmul(p_logits[:, t * E:(t + 1) * E], x3T[:, :], gate[:, :], start=True, stop=True).then_inc(s_gate, 1)
            now, pair = placing(h, c)
            if now:
                nc.tensor.wait_ge(s_onehot, pair + 1)
                mm = nc.tensor.matmul(p_place, before_bf[:, :], onehot[:, :, :].rearrange("p g e -> p (g e)"), start=True, stop=False,
                                      skip_group_check=True)
                for g in range(2 * TOPK):
                    mm = nc.tensor.matmul(p_place[:, (g + 1) * E:], ones_bf[:, :],
                                          onehot[:, g:g + 1, :].to_broadcast([P, 2 * TOPK - g, E]), start=False, stop=(g == 2 * TOPK - 1),
                                          skip_group_check=True)
                mm.then_inc(s_placed, 1)

        def route_bank(eng, h, c):
            now, pair = choosing(h, c)
            if now:
                eng.wait_ge(s_choose, CHOOSE_STEPS * pair + 1)
            now, pair = placing(h, c)
            if now:
                eng.wait_ge(s_begun, pair + 1)

        def route_act(h, c):
            if runs(h, c, -2):
                n = TURN * h + (c - 2)
                nc.scalar.wait_ge(s_x3Traw, n + 1)
                wait(nc.scalar, s_gate, n)
                nc.scalar.copy(x3T[:, :], p_x3T).then_inc(s_x3T, 1)

        def fill_rows(h, c):
            if runs(h, c, -4):
                n = TURN * h + (c - 4)
                t = c % 4
                if not isinstance(h, int) or c - 4 >= 4:
                    nc.scalar.wait_ge(s_sent[t], 32 * h + 32 * ((c - 4) // 4))
                nc.scalar.wait_ge(s_xn3, n + 1)
                nc.scalar.copy(row[:, t, :, 0:P], xn3[:, t:t + 1, :].to_broadcast([P, TOPK, P])).then_inc(s_rows, 1)

        def ratio_act(h, c):
            now, pair = choosing(h, c)
            if now:
                nc.scalar.wait_ge(s_choose, CHOOSE_STEPS * pair + 3)
                wait(nc.scalar, s_place, PLACE_STEPS * pair - PLACE_STEPS + 4)
                for t in range(2):
                    a = nc.scalar.activation(ratio[:, t, :], top[:, t, 0:1], ACT.Exp, bias=top[:, t, 1:2], scale=-1.0)
                a.then_inc(s_ratio, 1)

        def route_pool(h, c):
            if runs(h, c, -6):
                t = (c - 6) % 4
                nc.gpsimd.wait_ge(s_slot, TURN // 2 * h + (c - 6) // 2 + 1)
                nc.gpsimd.wait_ge(s_rows, TURN * h + (c - 6) + 1)
                plain(nc.gpsimd)
                for k in range(TOPK):
                    nc.gpsimd.indirect_dma_start(out=sent, out_offset=bass.IndirectOffsetOnAxis(ap=slot_u[:, t, k:k + 1], axis=0),
                                                 in_=row[:, t, k, :], in_offset=None).then_inc(s_sent[t], 16)

        def route_dve_bank(h, c):
            V = nc.vector
            now, pair = choosing(h, c)
            if now:
                V.wait_ge(s_gate, 2 * pair + 2)
                V.tensor_copy(logits[:, :, :], p_logits.rearrange("p (t e) -> p t e", t=2)).then_inc(s_choose, 1)
            now, pair = placing(h, c)
            if now:
                V.wait_ge(s_placed, pair + 1)
                wait(V, s_begun, pair)
                V.tensor_tensor(place[:, :, :], begin[:, :].unsqueeze(1).to_broadcast([P, 2 * TOPK, E]),
                                p_place[:, 0:2 * TOPK * E].rearrange("p (g e) -> p g e", e=E), ALU.add).then_inc(s_place, 1)
                V.wait_ge(s_place, PLACE_STEPS * pair + 1)
                V.tensor_tensor(begin[:, :], begin[:, :], p_total, ALU.add).then_inc(s_begun, 1)

        def route_dve(h, c):
            V = nc.vector
            now, pair = choosing(h, c)
            if now:
                def done(op):
                    op.then_inc(s_choose, 1)

                def needs(j):
                    V.wait_ge(s_choose, CHOOSE_STEPS * pair + j)
                needs(1)
                wait(V, s_ratio, pair)
                plain(V)
                done(V.max(top[:, 0, :], logits[:, 0, :]))
                done(V.max(top[:, 1, :], logits[:, 1, :]))
                needs(3)
                plain(V)
                done(V.max_index(top_at[:, 0, :], top[:, 0, :], logits[:, 0, :]))
                done(V.max_index(top_at[:, 1, :], top[:, 1, :], logits[:, 1, :]))
                needs(5)
                done(V.tensor_copy(top_atf[:, :, :], top_at[:, :, 0:TOPK]))
                needs(6)
                wait(V, s_placed, pair)
                V.tensor_tensor(onehot[:, 0:2 * TOPK, :], cv(C_IOTA, E).unsqueeze(1).to_broadcast([P, 2 * TOPK, E]),
                                top_atf[:, :, :].rearrange("p t k -> p (t k)").unsqueeze(2).to_broadcast([P, 2 * TOPK, E]),
                                ALU.is_equal).then_inc(s_onehot, 1)
            now, pair = placing(h, c)
            if now:
                def done(op):
                    op.then_inc(s_place, 1)

                def needs(j):
                    V.wait_ge(s_place, PLACE_STEPS * pair + j)
                V.wait_ge(s_ratio, pair + 1)
                done(V.tensor_scalar(ratio1[:, :, :], ratio[:, :, :], 1.0, None, ALU.add))
                half = slice((c - 5) % 4, (c - 5) % 4 + 2)
                if not isinstance(h, int) or c - 5 >= 4:
                    for t in range(half.start, half.stop):
                        V.wait_ge(s_sent[t], 32 * h + 32 * ((c - 5) // 4))
                needs(2)
                done(V.reciprocal(row[:, half, 0, P:P + 1], ratio1[:, :, :]))
                needs(3)
                done(V.tensor_tensor(row[:, half, 1, P:P + 1], row[:, half, 0, P:P + 1], ratio[:, :, :], ALU.mult))
                needs(1)
                V.wait_ge(s_onehot, pair + 1)
                done(V.tensor_tensor(mine[:, :, :], place[:, :, :], onehot[:, 0:2 * TOPK, :], ALU.mult))
                done(V.tensor_copy(row[:, half, :, P + 1:P + 2].squeeze(3), result_no[:, :, :]))
                needs(5)
                done(V.tensor_reduce(slot_f[:, :], mine[:, :, :], AX.X, ALU.add))
                needs(6)
                done(V.tensor_scalar(result_no[:, :, :], result_no[:, :, :], float(2 * P), None, ALU.add))
                needs(8)
                V.tensor_copy(slot_u[:, half, :].rearrange("p t k -> p (t k)"), slot_f[:, :]).then_inc(s_slot, 1)

        def route_table():
            V = nc.vector
            count = [0]

            def chain(op):
                op.then_inc(s_table, 1)
                count[0] += 1
                V.wait_ge(s_table, count[0])
            taken = begin[:, :]
            V.wait_ge(s_begun, B // 2)
            chain(V.tensor_scalar(pad_f[:, 0:E], taken, consts[:, C_ROWNO:C_ROWNO + 1], None, ALU.add))
            chain(V.tensor_scalar(pad_f[:, E:E + 1], consts[:, C_ROWNO:C_ROWNO + 1], float(E * CAP), None, ALU.add))
            V.tensor_copy(pad_u[:, :], pad_f[:, :]).then_inc(s_pads, 1)
            chain(V.tensor_tensor(nblocks[:, :], taken, cv(C_REGION, E), ALU.subtract))
            chain(V.tensor_scalar(count_i[:, :], nblocks[:, :], float(P - 1), None, ALU.add))
            chain(V.tensor_scalar(nblocks_i[:, :], count_i[:, :], 7, None, ALU.arith_shift_right))
            chain(V.tensor_copy(ends[:, 0, :], nblocks_i[:, :]))
            for s_, step in enumerate((1, 2, 4)):
                V.tensor_copy(ends[:, s_ + 1, 0:step], ends[:, s_, 0:step])
                chain(V.tensor_tensor(ends[:, s_ + 1, step:E], ends[:, s_, step:E], ends[:, s_, 0:E - step], ALU.add))
            chain(V.tensor_scalar(skip[:, :], ends[:, 0, :], -float(P), float(CAP), ALU.mult, ALU.add))
            number = cv(C_BLOCKNO, BLOCKS)
            chain(V.tensor_tensor(past[:, :, :], number.unsqueeze(2).to_broadcast([P, BLOCKS, E]),
                                  ends[:, 3:4, :].to_broadcast([P, BLOCKS, E]), ALU.is_ge))
            chain(V.tensor_reduce(block_f[:, 0, :], past[:, :, :], AX.X, ALU.add))
            chain(V.tensor_scalar(block_f[:, 0, :], block_f[:, 0, :], float(E - 1), float(F), ALU.min, ALU.mult))
            chain(V.tensor_tensor(past[:, :, :], past[:, :, :], skip[:, :].unsqueeze(1).to_broadcast([P, BLOCKS, E]), ALU.mult))
            chain(V.tensor_reduce(block_f[:, 1, :], past[:, :, :], AX.X, ALU.add))
            chain(V.scalar_tensor_tensor(out=block_f[:, 1, :], in0=number, scalar=float(P), in1=block_f[:, 1, :], op0=ALU.mult, op1=ALU.add))
            chain(V.tensor_scalar(block_f[:, 1, :], block_f[:, 1, :], float(E * CAP), None, ALU.min))
            V.tensor_copy(block_tab[:, :, :], block_f[:, :, :]).then_inc(s_tab, 1)

        LEAD = 4

        def expert_steps(eng, step):
            loop_from = U + 1
            turns = (BLOCKS - LEAD - loop_from) // U
            cols = {}
            for c in range(-2, loop_from):
                step(0, c, cols)
            with eng.Fori(0, turns) as h:
                cols = {}
                for c in range(loop_from, loop_from + U):
                    step(h, c, cols)
            cols = {}
            for c in range(loop_from + U * turns, BLOCKS + 1):
                step(0, c, cols)

        def block_there(h, c, lead):
            return not isinstance(h, int) or 0 <= c + lead < BLOCKS

        def table_at(which, i):
            return block_tab[0:1, which, bass.ds(i, 1)]

        def expert_pe(h, c, cols):
            n = U * h + c

            def col(lead):
                if c + lead not in cols:
                    cols[c + lead] = nc.tensor.value_load(table_at(0, n + lead), min_val=0, max_val=(E - 1) * F)
                return cols[c + lead]
            if block_there(h, c, 0):
                at = col(0)
                nc.tensor.wait_ge(s_gT, n + 1)
                wait(nc.tensor, s_gelu, n)
                nc.tensor.matmul(p_hidden[:, :], gotT[:, :], w1[:, bass.ds(at, F)], start=True, stop=True).then_inc(s_up, 1)
            if block_there(h, c, 1) and (not isinstance(h, int) or c >= 0) and c != 2 * U:
                col(1)
            if block_there(h, c, -1):
                at = col(-1)
                nc.tensor.wait_ge(s_hT, n)
                wait(nc.tensor, s_y, n - 1)
                for f in range(FC):
                    mm = nc.tensor.matmul(p_y, hiddenT[:, f, :], w2[:, bass.ds(at + f * P, P)], start=(f == 0), stop=(f == FC - 1))
                mm.then_inc(s_down, 1)
            if block_there(h, c, 1):
                nc.tensor.wait_ge(s_got[(c + 1) % U], 16 * h + 16 * ((c + 1) // U + 1))
                wait(nc.tensor, s_gT, n + 1)
                nc.tensor.transpose(p_gotT, got[:, (c + 1) % U, 0:P], ident).then_inc(s_gTraw, 1)
            if block_there(h, c, 0):
                nc.tensor.wait_ge(s_gelu, n + 1)
                wait(nc.tensor, s_hT, n)
                for f in range(FC):
                    mm = nc.tensor.transpose(p_hiddenT[:, f * P:(f + 1) * P], hidden[:, f * P:(f + 1) * P], ident)
                mm.then_inc(s_hTraw, 1)

        def read_rows(h, c, lead, n):
            slot = (c + lead) % U
            if not isinstance(h, int) or c + lead >= U:
                nc.scalar.wait_ge(s_y, n + lead + 1 - U)
            first = nc.scalar.value_load(table_at(1, n + lead), min_val=0, max_val=E * CAP)
            nc.scalar.dma_start(got[:, slot, :], sent[bass.ds(first, P), :]).then_inc(s_got[slot], 16)

        def expert_act(h, c, _):
            n = U * h + c
            if isinstance(h, int) and c == -2:
                for lead in range(2, LEAD + 1):
                    read_rows(h, c, lead, n)
            elif block_there(h, c, LEAD):
                read_rows(h, c, LEAD, n)
            if block_there(h, c, 0):
                nc.scalar.wait_ge(s_up, n + 1)
                wait(nc.scalar, s_hTraw, n)
                nc.scalar.activation(hidden[:, :], p_hidden[:, :], ACT.Gelu).then_inc(s_gelu, 1)
            if block_there(h, c, 1):
                nc.scalar.wait_ge(s_gTraw, n + 2)
                wait(nc.scalar, s_up, n + 1)
                nc.scalar.copy(gotT[:, :], p_gotT).then_inc(s_gT, 1)

        def expert_dve(h, c, _):
            n = U * h + c
            if block_there(h, c, -1):
                slot = (c - 1) % U
                nc.vector.wait_ge(s_down, n)
                if not isinstance(h, int) or c - 1 >= U:
                    nc.vector.wait_ge(s_back[slot], 16 * h + 16 * ((c - 1) // U))
                nc.vector.wait_ge(s_got[slot], 16 * h + 16 * ((c - 1) // U + 1))
                nc.vector.tensor_copy(result_at[:, slot:slot + 1], got[:, slot, P + 1:P + 2])
                nc.vector.tensor_scalar(weighted[:, slot, :], p_y, got[:, slot, P:P + 1], None, ALU.mult).then_inc(s_y, 1)
            if block_there(h, c, 0):
                nc.vector.wait_ge(s_hTraw, n + 1)
                wait(nc.vector, s_down, n)
                nc.vector.tensor_copy(hiddenT[:, :, :], p_hiddenT[:, :].rearrange("p (f t) -> p f t", t=P)).then_inc(s_hT, 1)

        def expert_pool(h, c, _):
            n = U * h + c
            if block_there(h, c, -1):
                slot = (c - 1) % U
                nc.gpsimd.wait_ge(s_y, n)
                plain(nc.gpsimd)
                nc.gpsimd.indirect_dma_start(out=results, out_offset=bass.IndirectOffsetOnAxis(ap=result_at[:, slot:slot + 1], axis=0),
                                             in_=weighted[:, slot, :], in_offset=None,
                                             bounds_check=TOPK * TOKENS - 1, oob_is_err=False).then_inc(s_back[slot], 16)

        kinds = [attention(0), attention(1)]

        @block.tensor
        def _(pe):
            pe.wait_ge(s_w, 16 * 6)
            pe.wait_ge(s_const, 6)
            pe.wait_ge(s_zero, 4)
            for k in range(min(parts, 2)):
                steps(pe, k, kinds[k][0])
            if parts > 2:
                pe.wait_ge(s_slot, B // 2)
                pe.wait_ge(s_moe_w, 32)
                pe.wait_ge(s_tab, 1)
                expert_steps(pe, expert_pe)

        @block.scalar
        def _(act):
            for k in range(min(parts, 2)):
                steps(act, k, kinds[k][1])
            if parts > 2:
                act.wait_ge(s_tab, 1)
                for slot in range(4):
                    act.wait_ge(s_sent[slot], 16 * TOPK * B // 4)
                act.wait_ge(s_padsent, 16 * (E + 1))
                expert_steps(act, expert_act)

        @block.gpsimd
        def _(pool):
            nc.gpsimd.memset(k_heads[:, :, :], 0.0).then_inc(s_zero, 1)
            pool.wait_ge(s_w, 16 * 6)
            pool.wait_ge(s_const, 8)
            pool.wait_ge(s_zero, 4)
            for k in range(min(parts, 2)):
                steps(pool, k, kinds[k][2])
            if parts > 2:
                pool.wait_ge(s_pads, 2)
                for e in range(E + 1):
                    nc.gpsimd.indirect_dma_start(out=sent, out_offset=bass.IndirectOffsetOnAxis(ap=pad_u[:, e:e + 1], axis=0),
                                                 in_=pad_row[:, :], in_offset=None).then_inc(s_padsent, 16)
                expert_steps(pool, expert_pool)

        @block.vector
        def _(dve):
            dve.wait_ge(s_w, 16 * 6)
            nc.vector.tensor_copy(ident_bf[:, :], ident).then_inc(s_const, 1)
            nc.vector.tensor_scalar(minus_ident_bf[:, :], ident, -1.0, None, ALU.mult).then_inc(s_const, 1)
            nc.vector.tensor_copy(masks_bf[:, :], cv(C_MASKS, 2 * WIN)).then_inc(s_const, 1)
            nc.vector.memset(eps[:, :], EPS).then_inc(s_const, 1)
            nc.vector.memset(minus_half[:, :], -0.5).then_inc(s_const, 1)
            nc.vector.memset(ones_bf[:, :], 1.0).then_inc(s_const, 1)
            nc.vector.tensor_copy(before_bf[:, :], cv(C_BEFORE, P)).then_inc(s_const, 1)
            nc.vector.memset(onehot[:, 2 * TOPK:, :], 0.0).then_inc(s_const, 1)
            nc.vector.memset(values[:, :, :, :, :], 0.0).then_inc(s_zero, 1)
            dve.wait_ge(s_zero, 2)
            every = values[:, :, :, :, :].rearrange("p s j m v -> p (s j m) v")
            nc.vector.memset(every[0:WIN, :, 2 * HD:2 * HD + 1], 1.0).then_inc(s_zero, 1)
            nc.vector.memset(every[WIN:P, :, 2 * HD + 1:VC], 1.0).then_inc(s_zero, 1)
            nc.vector.memset(mean_var[:, :, :], 1.0)
            nc.vector.memset(row[:, :, :, P + 2:ROW], 0.0)
            nc.vector.memset(pad_row[:, :], 0.0).then_inc(s_pads, 1)
            nc.vector.tensor_copy(begin[:, :], cv(C_REGION, E)).then_inc(s_const, 1)
            rowno = consts[:, C_ROWNO:C_ROWNO + 1]
            for t in range(2):
                for k in range(TOPK):
                    nc.vector.tensor_scalar(result_no[:, t, k:k + 1], rowno, float(k * TOKENS + t * P), None, ALU.add).then_inc(s_const, 1)
            dve.wait_ge(s_pads, 1)
            nc.vector.tensor_scalar(pad_row[:, P + 1:P + 2], rowno, float(TOPK * TOKENS), None, ALU.add).then_inc(s_const, 1)
            dve.wait_ge(s_const, 14)
            dve.wait_ge(s_x[0], 16)
            dve.wait_ge(s_x[1], 64)
            for k in range(min(parts, 2)):
                steps(dve, k, kinds[k][3])
            if parts > 2:
                route_table()
                expert_steps(dve, expert_dve)
                for t in range(B // CH):
                    dve.wait_ge(s_read[t % 2], 32 * (t // 2 + 1))
                    for k in range(TOPK):
                        part = x[:, t * CH * P:(t + 1) * CH * P].rearrange("p (b d) -> p b d", d=P)
                        if k:
                            dve.wait_ge(s_sum, TOPK * t + k)
                        nc.vector.tensor_tensor(part, part, back[:, t % 2, k, :, :], ALU.add).then_inc(s_sum, 1)


def laid_out(i):
    f = lambda a: np.asarray(a)
    qkv, wo = f(i["L0_attn_w_qkv"]), f(i["L0_attn_w_out"])
    half = np.arange(P).reshape(HEADS, 2, HD // 2)[:, ::-1].reshape(-1)
    q, k, v = qkv[0:P], qkv[P:2 * P], qkv[2 * P:]
    order = np.concatenate([np.arange(b * BLK, (b + 1) * BLK) for b in BLOCK_ORDER])
    c = np.ascontiguousarray
    return {
        "x_in": c(f(i["x"])),
        "ctxT_in": c(f(i["ctx_1024"])[:, order].transpose(0, 2, 1)),
        "consts_in": shape_constants(),
        "wself_in": c(np.concatenate([q.T, q[half].T, k.T, k[half].T, v.T, wo.T], axis=1)),
        "wcross_in": c(np.concatenate([f(i["L0_xattn_W" + s]).T for s in "qkvo"], axis=1)),
        "cols_in": c(np.stack([f(i["L0_xattn_bq"]), f(i["L0_xattn_bk"])], axis=1)),
        "rows_in": c(np.concatenate([f(i["L0_xattn_bv"]), f(i["L0_xattn_bo"])])),
        "gate_in": c(f(i["L0_ffn_gate_w"])),
        "w1_in": c(f(i["L0_ffn_w1"]).transpose(1, 0, 2).reshape(P, E * F)),
        "w2_in": c(f(i["L0_ffn_w2"]).reshape(E, FC, P, P).transpose(2, 0, 1, 3).reshape(P, E * F)),
    }


def kernel(**inputs):
    import concourse.bacc as _bacc
    from concourse.bass_utils import run_bass_kernel_spmd as _run

    nc = _bacc.Bacc("TRN2", target_bir_lowering=False, num_devices=1)
    arrays = laid_out(inputs)
    args = [nc.dram_tensor(n, a.shape, mybir.dt.from_np(a.dtype), kind="ExternalInput").ap() for n, a in arrays.items()]
    out = nc.dram_tensor("out", (B, P, P), mybir.dt.float32, kind="ExternalOutput").ap()
    build(nc, *args, out)
    r = _run(nc, [arrays], core_ids=[0])
    return r.results[0]["out"]
```

```python
import math
from itertools import zip_longest

import numpy as np

import concourse.bass as bass
from concourse import mybir

P = 128
B = 32
HEADS, HD = 16, 8
BLK = 32
NBLK = P // BLK
G = 4
NG = HEADS // G
WIN = 2 * BLK
PAIRS = HEADS // 2
VC = 2 * HD + 2
SELF_WINDOW, CROSS_WINDOW = 32, 16
SCALE = 1.0 / math.sqrt(HD)
EPS = 1e-5
MASKED = -1e30

E, F, TOPK = 8, 512, 2
FC = F // P
TOKENS = B * P
CAP = TOKENS + P
ROW = P + 4
BLOCKS = (TOKENS * TOPK + E * (P - 1)) // P
U = 8

C_IDENT = 0
C_COS = C_IDENT + P
C_SIN = C_COS + 2 * P
C_MASKS = C_SIN + 2 * P
C_HEAD = C_MASKS + 2 * WIN
C_GROUP = C_HEAD + G
C_BEFORE = C_GROUP + NG
C_IOTA = C_BEFORE + P
C_ROWNO = C_IOTA + E
C_REGION = C_ROWNO + 1
C_END = C_REGION + E

KEYS_OF = [(0, None), (0, 1), (2, 1), (2, 3)]
BLOCK_ORDER = (0, 2, 1, 3)


def shape_constants():
    c = np.zeros((P, C_END), np.float32)
    c[:, C_IDENT:C_IDENT + P] = np.eye(P)
    inv = (1.0 / np.float32(10000.0) ** (np.arange(0, HD, 2, dtype=np.float32) / np.float32(HD))).astype(np.float32)
    ang = (np.arange(P, dtype=np.float32)[:, None] * inv[None, :]).astype(np.float32)
    cos, sin = np.cos(ang).astype(np.float32), np.sin(ang).astype(np.float32)
    feat = np.arange(P) % HD
    cosT = cos.T[feat % (HD // 2)]
    sinT = sin.T[feat % (HD // 2)] * np.where(feat < HD // 2, -1.0, 1.0)[:, None]
    order = np.concatenate([np.arange(b * BLK, (b + 1) * BLK) for b in BLOCK_ORDER])
    c[:, C_COS:C_COS + P], c[:, C_COS + P:C_COS + 2 * P] = cosT, cosT[:, order]
    c[:, C_SIN:C_SIN + P], c[:, C_SIN + P:C_SIN + 2 * P] = sinT, sinT[:, order]
    for q in range(P):
        for slot in range(2):
            block = KEYS_OF[q // BLK][slot]
            for k in range(BLK):
                if block is None:
                    own, cross = False, k < min(q + 1, CROSS_WINDOW - 1 - q)
                else:
                    key = block * BLK + k
                    own = key <= q and q - key < SELF_WINDOW
                    cross = key <= q and q - key < CROSS_WINDOW and key - (q - CROSS_WINDOW + 1) <= q
                for n, allowed in enumerate((own, cross)):
                    c[q, C_MASKS + n * WIN + slot * BLK + k] = 0.0 if allowed else MASKED
    for p in range(P):
        c[p, C_HEAD + (p // HD) % G] = 1.0
        c[p, C_GROUP + p // (G * HD)] = 1.0
        c[p, C_BEFORE + p + 1:C_BEFORE + P] = 1.0
        c[p, C_IOTA:C_IOTA + E] = np.arange(E)
        c[p, C_ROWNO] = p
        c[p, C_REGION:C_REGION + E] = np.arange(E) * CAP
    return c


def build(nc, x_in, ctxT_in, consts_in, wself_in, wcross_in, cols_in, rows_in, gate_in, w1_in, w2_in, out):
    from contextlib import ExitStack
    F32, BF16, I32, U32 = mybir.dt.float32, mybir.dt.bfloat16, mybir.dt.int32, mybir.dt.uint32
    ALU, ACT, AX = mybir.AluOpType, mybir.ActivationFunctionType, mybir.AxisListType

    ctx = ExitStack()
    with ctx:
        def sb(name, shape, dt=F32):
            return ctx.enter_context(nc.sbuf_tensor(name, shape, dt))

        def pb(name):
            return ctx.enter_context(nc.psum_tensor(name, [P, 512], F32))

        def sem(name):
            return ctx.enter_context(nc.semaphore(name))

        sent = nc.dram_tensor("sent_rows", [(E + 1) * CAP, ROW], F32, kind="Internal").ap()
        results = nc.dram_tensor("expert_results", [TOPK * TOKENS, P], F32, kind="Internal").ap()

        x = sb("x", [P, B * P])
        consts = sb("consts", [P, C_END])
        wself = sb("wself", [P, 6 * P])
        wcross = sb("wcross", [P, 4 * P])
        cols = sb("cols", [P, 2])
        rows = sb("rows", [P, 2 * P])
        gate = sb("gate", [P, E])
        w1 = sb("w1", [P, E * F])
        w2 = sb("w2", [P, E * F])
        ident_bf = sb("ident_bf", [P, P], BF16)
        minus_ident_bf = sb("minus_ident_bf", [P, P], BF16)
        masks_bf = sb("masks_bf", [P, 2 * WIN], BF16)
        ones_bf = sb("ones_bf", [P, P], BF16)
        before_bf = sb("before_bf", [P, P], BF16)

        stats = sb("stats", [P, 2, 6])
        mean_var = sb("mean_var", [P, 2, 2])
        eps = sb("eps", [P, 1])
        minus_half = sb("minus_half", [P, 1])
        var_eps = sb("var_eps", [P, 2])
        rstd = sb("rstd", [P, 2])
        xn = sb("xn", [P, 2, P])
        xnT = sb("xnT", [P, 2, P])
        ctxT = sb("ctxT", [P, 2, P])
        turned_cos = sb("turned_cos", [P, 2, P])
        turned_sin = sb("turned_sin", [P, 2, P])
        qk = sb("qk", [P, 2, P])
        q_groups = sb("q_groups", [P, NG, P])
        k_heads = sb("k_heads", [P, G, P + BLK])
        shift = sb("shift", [P, HEADS], BF16)
        peak = sb("peak", [P, HEADS])
        lowered = sb("lowered", [P, HEADS, WIN])
        probs = sb("probs", [P, HEADS * WIN])
        probsT = sb("probsT", [P, PAIRS, P])
        values = sb("values", [P, 4, NBLK, PAIRS, VC])
        inv_sum = sb("inv_sum", [P, PAIRS, 2])
        att = sb("att", [P, P])
        attT = sb("attT", [P, P])

        p_scores = [pb("p_scores0"), pb("p_scores1")]
        p_probsT = [pb("p_probsT0"), pb("p_probsT1")]
        p_qk, p_v, p_att, p_misc = pb("p_qk"), pb("p_v"), pb("p_att"), pb("p_misc")
        p_xT, p_attT, p_proj = p_misc[:, 0:P], p_misc[:, P:2 * P], p_misc[:, 2 * P:3 * P]

        row = sb("row", [P, 4, TOPK, ROW])
        xn3 = sb("xn3", [P, 4, P])
        x3T = sb("x3T", [P, P])
        logits = sb("logits", [P, 2, E])
        top = sb("top", [P, 2, 8])
        top_at = sb("top_at", [P, 2, 8], U32)
        top_atf = sb("top_atf", [P, 2, TOPK])
        ratio = sb("ratio", [P, 2, 1])
        ratio1 = sb("ratio1", [P, 2, 1])
        onehot = sb("onehot", [P, 2 * TOPK + 1, E], BF16)
        begin = sb("begin", [P, E])
        place = sb("place", [P, 2 * TOPK, E])
        mine = sb("mine", [P, 2 * TOPK, E])
        slot_f = sb("slot_f", [P, 2 * TOPK])
        slot_u = sb("slot_u", [P, 4, TOPK], U32)
        result_no = sb("result_no", [P, 2, TOPK])
        pad_row = sb("pad_row", [P, ROW])
        region_end = sb("region_end", [P, E], I32)
        count_i = sb("count_i", [P, E], I32)
        nblocks_i = sb("nblocks_i", [P, E], I32)
        nblocks = sb("nblocks", [P, E])
        ends = sb("ends", [P, 4, E])
        skip = sb("skip", [P, E])
        past = sb("past", [P, 2, E])
        block_sum = sb("block_sum", [P, 2])
        block_f = sb("block_f", [P, 2])
        block_tab = sb("block_tab", [P, 2, BLOCKS], I32)
        p_x3T, p_block = p_qk[:, 3 * P:4 * P], p_probsT[0][:, 0:2 * P]
        p_logits, p_place, p_total = p_att[:, 160:160 + 2 * E], p_att[:, 192:192 + (2 * TOPK + 1) * E], p_att[:, 192 + 2 * TOPK * E:192 + (2 * TOPK + 1) * E]

        got = sb("got", [P, U, ROW])
        w1_now = sb("w1_now", [P, 2, F])
        w2_now = sb("w2_now", [P, 2, F])
        gotT = sb("gotT", [P, 2, P])
        hidden = sb("hidden", [P, 2, F])
        weighted = sb("weighted", [P, U, P])
        result_at = sb("result_at", [P, U], U32)
        p_gotT, p_hidden, p_y = [p_misc[:, 0:P], p_qk[:, 0:P]], p_scores, [p_att[:, 0:P], p_v[:, 0:P]]

        CH = 4
        back = sb("back", [P, B // CH, TOPK, CH, P])

        s_x = [sem(f"x_loaded{i}") for i in range(2)]
        s_consts, s_wself, s_w = sem("constants_loaded"), sem("self_weights_loaded"), sem("weights_loaded")
        s_moe_w = sem("expert_weights_loaded")
        s_const = sem("constants_made")
        s_zero = sem("buffers_cleared")
        s_ctx = [sem(f"ctx_loaded{i}") for i in range(2)]
        s_stats, s_mv, s_ve, s_rstd = sem("stats_made"), sem("mean_var_made"), sem("var_eps_made"), sem("rstd_made")
        s_xn, s_xTraw, s_xT = sem("xn_made"), sem("xT_in_psum"), sem("xT_made")
        s_bo = sem("bo_added")
        s_qkraw, s_rot, s_qk = sem("qk_in_psum"), sem("rotary_parts"), sem("qk_made")
        s_spread = sem("qk_spread")
        s_scores, s_max, s_shifted = sem("scores_made"), sem("max_made"), sem("scores_shifted")
        s_masked = sem("scores_masked_by_dve")
        s_grouped = sem("q_grouped")
        s_probs, s_pTraw, s_pT = sem("probs_made"), sem("probsT_in_psum"), sem("probsT_made")
        s_vraw, s_v = sem("v_in_psum"), sem("v_made")
        s_attraw, s_inv, s_att = sem("att_in_psum"), sem("sums_inverted"), sem("att_made")
        s_aTraw, s_aT, s_proj, s_res = sem("attT_in_psum"), sem("attT_made"), sem("proj_in_psum"), sem("x_updated")

        s_st3, s_xn3, s_x3Traw, s_x3T = sem("stats3_made"), sem("xn3_made"), sem("x3T_in_psum"), sem("x3T_made")
        s_rows, s_gate, s_ratio = sem("rows_filled"), sem("gate_in_psum"), sem("ratio_made")
        s_choose, s_onehot, s_placed = sem("choosing_steps"), sem("onehot_made"), sem("places_in_psum")
        s_place, s_slot, s_begun = sem("placing_steps"), sem("slots_made"), sem("begin_moved")
        s_sent = [sem(f"rows_sent{i}") for i in range(4)]
        s_pads, s_padsent, s_table, s_tab = sem("pads_made"), sem("pads_sent"), sem("table_steps"), sem("table_made")
        s_block, s_blockT = sem("table_on_partitions"), sem("table_in_psum")
        s_got = [sem(f"rows_got{i}") for i in range(U)]
        s_back = [sem(f"results_sent{i}") for i in range(U)]
        s_gTraw, s_gT, s_up, s_gelu = sem("gotT_in_psum"), sem("gotT_made"), sem("hidden_in_psum"), sem("hidden_made")
        s_w1_now, s_w2_now, s_down, s_y = sem("w1_copied"), sem("w2_copied"), sem("y_in_psum"), sem("y_weighted")
        s_read = [sem(f"results_read{i}") for i in range(B // CH)]
        s_plain = sem("waits_standing_alone")
        s_sum, s_sum_pool, s_out = sem("results_added"), sem("results_added_by_pool"), sem("out_written")

        block = ctx.enter_context(nc.Block())

        def cv(at, n):
            return consts[:, at:at + n]

        def x_of(n):
            return x[:, bass.ts(n, P)]

        ident = cv(C_IDENT, P)

        def key_step(j):
            first, second = KEYS_OF[j]
            at = BLOCK_ORDER.index(first)
            return at, (NBLK if second is None else BLOCK_ORDER.index(second)) - at

        def pair_of_blocks(tile, j):
            at, step = key_step(j)
            v = tile.rearrange("p h (b k) -> p h b k", k=BLK)
            return v[:, :, at:at + step + 1:step, :]

        FIRST = -5
        TURN = 4
        LOOP_FROM = (2, 8)
        LAST = (B, B + 5)

        def emit(*steps_at_once):
            for _ in zip_longest(*steps_at_once):
                pass

        def attend(eng, self_step, cross_step):
            def looped(step, first, loop_from, end):
                turns = (B - 5 - loop_from) // TURN
                for c in range(first, loop_from):
                    emit(step(0, c))
                with eng.Fori(0, turns) as h:
                    for c in range(loop_from, loop_from + TURN):
                        emit(step(h, c))
                for c in range(loop_from + TURN * turns, end):
                    emit(step(0, c))
            looped(self_step, FIRST, LOOP_FROM[0], B + FIRST)
            eng.wait_ge(s_w, 16 * 4)
            for c in range(B + FIRST, LAST[0] + 1):
                emit(self_step(0, c), cross_step(0, c - B))
            looped(cross_step, LAST[0] + 1 - B, LOOP_FROM[1], LAST[1] + 1)

        def runs(h, c, lead):
            return not isinstance(h, int) or 0 <= c + lead < B

        def wait(eng, s, value):
            if not isinstance(value, int) or value > 0:
                eng.wait_ge(s, value)

        def plain(eng):
            eng.sem_inc(s_plain, 1)

        POOL_CHUNKS = (2, 5)
        DVE_CHUNKS = tuple(t for t in range(B // CH) if t not in POOL_CHUNKS)

        def add_results(eng, compute, chunks, s_added):
            for m, t in enumerate(chunks):
                part = x[:, t * CH * P:(t + 1) * CH * P].rearrange("p (b d) -> p b d", d=P)
                eng.wait_ge(s_read[t], 16 * TOPK)
                for k in range(TOPK):
                    if k:
                        eng.wait_ge(s_added, TOPK * m + k)
                    compute.tensor_tensor(part, part, back[:, t, k, :, :], ALU.add).then_inc(s_added, 1)

        def send_pads(eng, experts):
            eng.wait_ge(s_pads, 3)
            for e in experts:
                first = eng.value_load(region_end[0:1, e:e + 1], min_val=e * CAP, max_val=(e + 1) * CAP - P)
                eng.dma_start(sent[bass.ds(first, P), :], pad_row[:, :]).then_inc(s_padsent, 16)

        @block.sync
        def _(sp):
            xv = x_in.rearrange("b s d -> s b d")
            xs = x[:, :].rearrange("p (b d) -> p b d", d=P)
            sp.dma_start(xs[:, 0:4, :], xv[:, 0:4, :]).then_inc(s_x[0], 16)
            sp.dma_start(wself[:, :], wself_in).then_inc(s_wself, 16)
            for b in (4, 11, 18, 25):
                sp.dma_start(xs[:, b:b + 7, :], xv[:, b:b + 7, :]).then_inc(s_x[1], 16)
            sp.dma_start(w1[:, :], w1_in).then_inc(s_moe_w, 16)
            sp.dma_start(w2[:, :], w2_in).then_inc(s_moe_w, 16)
            for slot in range(2):
                sp.dma_start(ctxT[:, slot, :], ctxT_in[slot]).then_inc(s_ctx[slot], 16)
            sp.wait_ge(s_pads, 2)
            sp.dma_start(sent[E * CAP:E * CAP + P, :], pad_row[:, :]).then_inc(s_padsent, 16)
            with sp.Fori(1, B // 2) as h:
              for slot in range(2):
                  sp.wait_ge(s_vraw, 2 * h + (B + slot - 1))
                  sp.dma_start(ctxT[:, slot, :], ctxT_in[bass.ds(2 * h + slot, 1)].rearrange("o p t -> (o p) t")).then_inc(s_ctx[slot], 16)
            send_pads(sp, range(E // 2))
            for slot in range(U):
                sp.wait_ge(s_back[slot], 16 * len(range(slot, BLOCKS, U)))
            rv = results.rearrange("(n s) d -> s n d", s=P)
            ov = out.rearrange("b s d -> s b d")

            for t in range(B // CH):
                for k in range(TOPK):
                    sp.dma_start(back[:, t, k, :, :], rv[:, k * B + t * CH:k * B + (t + 1) * CH, :]).then_inc(s_read[t], 16)
            for t in range(B // CH):
                if t in POOL_CHUNKS:
                    sp.wait_ge(s_sum_pool, TOPK * (POOL_CHUNKS.index(t) + 1))
                else:
                    sp.wait_ge(s_sum, TOPK * (DVE_CHUNKS.index(t) + 1))
                sp.dma_start(ov[:, t * CH:(t + 1) * CH, :], xs[:, t * CH:(t + 1) * CH, :]).then_inc(s_out, 16)
            sp.wait_ge(s_out, 16 * (B // CH))

        def attention(kind):
            base = B * kind
            own = kind == 0
            act_groups = 3 if own else 2
            w = wself if own else wcross
            wq, wqr, wk, wkr, wv, wo = (
                [w[:, i * P:(i + 1) * P] for i in range(6)] if own
                else [w[:, 0:P], None, w[:, P:2 * P], None, w[:, 2 * P:3 * P], w[:, 3 * P:4 * P]])

            def dve_masks(half):
                return own and half == 1

            def exists(h, c, lead):
                return not isinstance(h, int) or 0 <= base + c + lead < 2 * B

            def take_values(eng, h, c):
                if runs(h, c, 2):
                    n = TURN * h + (c + 2 + base)
                    slot = (c + 2) % 4
                    eng.wait_ge(s_vraw, n + 1)
                    wait(eng, s_attraw, n - 3)
                    if n_is_first(n):
                        eng.wait_ge(s_zero, 3)
                    for t in range(2):
                        for key_slot in range(2):
                            lo = t * WIN + key_slot * BLK
                            for v in range(2):
                                js = [j for j in range(NBLK) if KEYS_OF[j][key_slot] == 2 * v + key_slot]
                                src = p_v[lo:lo + BLK, v * P:(v + 1) * P].rearrange("p (m t d) -> p m t d", t=2, d=HD)[:, :, t, :]
                                src = src.unsqueeze(1).to_broadcast([BLK, len(js), PAIRS, HD])
                                dst = values[lo:lo + BLK, slot, js[0]:js[-1] + 1, :, t * HD:(t + 1) * HD]
                                if own:
                                    a = nc.scalar.copy(dst, src)
                                else:
                                    bv = rows[lo:lo + BLK, 0:P].rearrange("p (m t d) -> p m t d", t=2, d=HD)[:, :, t, :]
                                    a = nc.vector.tensor_tensor(dst, src, bv.unsqueeze(1).to_broadcast([BLK, len(js), PAIRS, HD]), ALU.add)
                    a.then_inc(s_v, 1)

            def project(h, c):
                if runs(h, c, -1):
                    n = TURN * h + (c - 1 + base)
                    nc.tensor.wait_ge(s_aT, n + 1)
                    nc.tensor.matmul(p_proj, attT[:, :], wo, start=True, stop=True).then_inc(s_proj, 1)

            def pe_step(h, c):
                def at(lead):
                    return TURN * h + (c + lead)

                def count(lead):
                    return TURN * h + (c + lead + base)
                if runs(h, c, 1):
                    n = count(1)
                    for r in range(NG):
                        half = r // 2
                        if r % 2 == 0:
                            if n_of_self(n):
                                wait(nc.tensor, s_masked if half else s_shifted, n if half else 2 * n - 1)
                            else:
                                wait(nc.tensor, s_probs, 2 * n - 1 + half)
                            if not dve_masks(half):
                                nc.tensor.matmul(p_scores[half][:, :], ident_bf[:, :],
                                                 masks_bf[:, kind * WIN:(kind + 1) * WIN].unsqueeze(1).to_broadcast([P, HEADS // 2, WIN]),
                                                 start=True, stop=False, skip_group_check=True)
                        if r == 0:
                            nc.tensor.wait_ge(s_spread, n + 1)
                            nc.tensor.wait_ge(s_grouped, n + 1)
                        for j in range(NBLK):
                            out_ = p_scores[r // 2][j * BLK:(j + 1) * BLK, (r % 2) * G * WIN:(r % 2 + 1) * G * WIN]
                            mm = nc.tensor.matmul(out_, q_groups[:, r, j * BLK:(j + 1) * BLK],
                                                  pair_of_blocks(k_heads[:, :, :], j),
                                                  start=dve_masks(r // 2), stop=dve_masks(r // 2) or r % 2 == 1, skip_group_check=True)
                        if r % 2 == 1:
                            mm.then_inc(s_scores, 1)
                yield
                if runs(h, c, -1):
                    n = count(-1)
                    nc.tensor.wait_ge(s_att, n + 1)
                    wait(nc.tensor, s_aT, n)
                    wait(nc.tensor, s_res, n)
                    if exists(h, c, 2):
                        nc.tensor.wait_ge(s_xT, count(2) + 1)
                    nc.tensor.transpose(p_attT, att[:, :], ident).then_inc(s_aTraw, 1)
                yield
                if runs(h, c, 2):
                    n = count(2)
                    nc.tensor.wait_ge(s_xT, n + 1)
                    wait(nc.tensor, s_qk, n)
                    if not own and runs(h, c, -3):
                        nc.tensor.wait_ge(s_x3T, at(-3) + 1)
                    q_tokens = xnT[:, (c + 2) % 2, :].rearrange("p (lo hi k) -> p hi lo k", lo=2, k=BLK)
                    if own:
                        nc.tensor.matmul(p_qk[:, 0:P], wq, q_tokens, start=True, stop=True)
                        nc.tensor.matmul(p_qk[:, P:2 * P], wk, xnT[:, (c + 2) % 2, :], start=True, stop=True)
                        nc.tensor.matmul(p_qk[:, 2 * P:3 * P], wqr, q_tokens, start=True, stop=True)
                        nc.tensor.matmul(p_qk[:, 3 * P:4 * P], wkr, xnT[:, (c + 2) % 2, :], start=True, stop=True).then_inc(s_qkraw, 1)
                    else:
                        slot = (c + 2) % 2
                        nc.tensor.matmul(p_qk[:, 0:P], wq, q_tokens, start=True, stop=True)
                        nc.tensor.wait_ge(s_ctx[slot], 8 * TURN * h + 16 * ((c + 2) // 2 + 1))
                        nc.tensor.matmul(p_qk[:, P:2 * P], wk, ctxT[:, slot, :], start=True, stop=True).then_inc(s_qkraw, 1)
                yield
                if own:
                    project(h, c)
                else:
                    route_pe(h, c)
                yield
                if runs(h, c, 0):
                    n = count(0)
                    for m in range(PAIRS):
                        if m % 4 == 0:
                            nc.tensor.wait_ge(s_probs, 2 * n + 1 + m // 4)
                            wait(nc.tensor, s_pT, 2 * n - 1 + m // 4)
                        mm = nc.tensor.transpose(p_probsT[m // 4][:, (m % 4) * P:(m % 4 + 1) * P],
                                                 probs[:, m * P:(m + 1) * P], ident)
                        if m % 4 == 3:
                            mm.then_inc(s_pTraw, 1)
                if not own:
                    project(h, c)
                yield
                if runs(h, c, 2):
                    n = count(2)
                    wait(nc.tensor, s_v, n)
                    src = xnT[:, (c + 2) % 2, :] if own else ctxT[:, (c + 2) % 2, :]
                    for v in range(2):
                        for quarter in range(4):
                            pos = BLOCK_ORDER.index(2 * v + quarter % 2)
                            mm = nc.tensor.matmul(p_v[quarter * BLK:(quarter + 1) * BLK, v * P:(v + 1) * P],
                                                  src[:, pos * BLK:(pos + 1) * BLK], wv, start=True, stop=True)
                    mm.then_inc(s_vraw, 1)
                yield
                if not own and runs(h, c, 1):
                    n = count(1)
                    for half in range(2):
                        nc.tensor.wait_ge(s_max, 2 * n + 1 + half)
                        mm = nc.tensor.matmul(p_scores[half][:, :], minus_ident_bf[:, :],
                                              shift[:, half * 8:half * 8 + 8].unsqueeze(2).to_broadcast([P, 8, WIN]),
                                              start=False, stop=True, skip_group_check=True)
                        mm.then_inc(s_shifted, 1)
                yield
                if runs(h, c, 3):
                    n = count(3)
                    nc.tensor.wait_ge(s_xn, n + 1)
                    wait(nc.tensor, s_xT, n)
                    wait(nc.tensor, s_res, count(0) if exists(h, c, -1) else 0)
                    nc.tensor.transpose(p_xT, xn[:, (c + 3) % 2, :], ident).then_inc(s_xTraw, 1)
                yield
                if not own and runs(h, c, -2):
                    n = at(-2)
                    nc.tensor.wait_ge(s_xn3, n + 1)
                    wait(nc.tensor, s_x3T, n)
                    if runs(h, c, 2):
                        nc.tensor.wait_ge(s_qk, count(2) + 1)
                    nc.tensor.transpose(p_x3T, xn3[:, (c - 2) % 4, :], ident).then_inc(s_x3Traw, 1)
                yield
                if runs(h, c, 0):
                    n = count(0)
                    slot = c % 4
                    nc.tensor.wait_ge(s_v, n + 1)
                    wait(nc.tensor, s_att, n)
                    if not own:
                        route_bank(nc.tensor, h, c)
                    for m in range(PAIRS):
                        if m % 4 == 0:
                            nc.tensor.wait_ge(s_pT, 2 * n + 1 + m // 4)
                        for j in range(NBLK):
                            mm = nc.tensor.matmul(p_att[j * BLK:(j + 1) * BLK, m * VC:(m + 1) * VC],
                                                  probsT[:, m, j * BLK:(j + 1) * BLK], values[:, slot, j, m, :],
                                                  start=True, stop=True)
                    mm.then_inc(s_attraw, 1)

            def act_step(h, c):
                def count(lead):
                    return TURN * h + (c + lead + base)
                if runs(h, c, -1):
                    n = count(-1)
                    nc.scalar.wait_ge(s_aTraw, n + 1)
                    wait(nc.scalar, s_proj, n)
                    nc.scalar.copy(attT[:, :], p_attT).then_inc(s_aT, 1)
                yield
                if not own and runs(h, c, 2):
                    n = count(2)
                    nc.scalar.wait_ge(s_qkraw, n + 1)
                    wait(nc.scalar, s_spread, n)
                    nc.scalar.activation(qk[:, 1, :], p_qk[:, P:2 * P], ACT.Identity, bias=cols[:, 1:2])
                    nc.scalar.activation(qk[:, 0, :], p_qk[:, 0:P], ACT.Identity, bias=cols[:, 0:1]).then_inc(s_qk, 1)
                yield
                if runs(h, c, 0):
                    n = count(0)
                    wait(nc.scalar, s_attraw, n)
                    for half in range(2):
                        nc.scalar.wait_ge(s_pTraw, 2 * n + 1 + half)
                        nc.scalar.copy(probsT[:, 4 * half:4 * half + 4, :],
                                       p_probsT[half][:, :].rearrange("p (m q) -> p m q", q=P)).then_inc(s_pT, 1)
                if runs(h, c, 2):
                    n = count(2)
                    nc.scalar.wait_ge(s_qk, n + 1)
                    wait(nc.scalar, s_scores, 2 * n)
                    for r in range(act_groups):
                        a = nc.scalar.activation(q_groups[:, r, :], qk[:, 0, :], ACT.Identity, scale=cv(C_GROUP + r, 1))
                    a.then_inc(s_grouped, 1)
                yield
                if runs(h, c, 1):
                    n = count(1)
                    for half in range(2):
                        nc.scalar.wait_ge(s_shifted, 2 * n + 1 + half)
                        wait(nc.scalar, s_pTraw, 2 * n - 1 + half)
                        nc.scalar.activation(probs[:, half * 512:half * 512 + 512],
                                             lowered[:, half * 8:half * 8 + 8, :].rearrange("p h k -> p (h k)") if own else p_scores[half][:, :],
                                             ACT.Exp, scale=SCALE).then_inc(s_probs, 1)
                yield
                if runs(h, c, 3):
                    n = count(3)
                    nc.scalar.wait_ge(s_xTraw, n + 1)
                    wait(nc.scalar, s_vraw, n - 1)
                    nc.scalar.copy(xnT[:, (c + 3) % 2, :].rearrange("p (lo hi k) -> p lo hi k", lo=2, k=BLK),
                                   p_xT.rearrange("p (hi lo k) -> p lo hi k", lo=2, k=BLK)).then_inc(s_xT, 1)
                if own:
                    take_values(nc.scalar, h, c)
                else:
                    fill_rows(h, c)
                    route_act(h, c)
                    ratio_act(h, c)

            def pool_step(h, c):
                def count(lead):
                    return TURN * h + (c + lead + base)
                if runs(h, c, 2):
                    n = count(2)
                    nc.gpsimd.wait_ge(s_qk, n + 1)
                    wait(nc.gpsimd, s_scores, 2 * n)
                    nc.gpsimd.tensor_tensor(k_heads[:, :, 0:P], qk[:, 1:2, :].to_broadcast([P, G, P]),
                                            cv(C_HEAD, G).unsqueeze(2).to_broadcast([P, G, P]), ALU.mult)
                    nc.gpsimd.tensor_tensor(q_groups[:, act_groups:, :], qk[:, 0:1, :].to_broadcast([P, NG - act_groups, P]),
                                            cv(C_GROUP + act_groups, NG - act_groups).unsqueeze(2).to_broadcast([P, NG - act_groups, P]),
                                            ALU.mult).then_inc(s_spread, 1)
                if not own and (not isinstance(h, int) or c <= B):
                    route_pool(h, c, [c - 6])
                yield
                if not own and runs(h, c, 4):
                    nc.gpsimd.wait_ge(s_xn, count(4) + 1)
                    nc.gpsimd.tensor_tensor(x_of(TURN * h + (c + 4)), x_of(TURN * h + (c + 4)), rows[:, P:2 * P], ALU.add).then_inc(s_bo, 1)
                yield
                if runs(h, c, 5) or (not own and runs(h, c, -1)):
                    n = count(5)
                    both = 1 if own else 2
                    nc.gpsimd.wait_ge(s_mv, n + 1)
                    if exists(h, c, 4):
                        wait(nc.gpsimd, s_xn, n)
                    if not own and runs(h, c, -2):
                        nc.gpsimd.wait_ge(s_xn3, TURN * h + (c - 1))
                    nc.gpsimd.tensor_tensor(var_eps[:, 0:both], mean_var[:, 0:both, 1:2].squeeze(2),
                                            eps[:, 0:1].to_broadcast([P, both]), ALU.add).then_inc(s_ve, 1)
                    nc.gpsimd.wait_ge(s_ve, n + 1)
                    nc.gpsimd.tensor_tensor(rstd[:, 0:both], var_eps[:, 0:both], minus_half[:, 0:1].to_broadcast([P, both]), ALU.pow).then_inc(s_rstd, 1)
                if not own and isinstance(h, int) and c >= B and c % 2 == 0:
                    route_pool(h, c, [c - 5] if c == B else [c - 6, c - 5])

            def add_result(h, c):
                if runs(h, c, -1):
                    n = TURN * h + (c - 1 + base)
                    nc.vector.wait_ge(s_proj, n + 1)
                    if not own:
                        nc.vector.wait_ge(s_bo, n - base + 1)
                    nc.vector.tensor_tensor(x_of(TURN * h + (c - 1)), x_of(TURN * h + (c - 1)), p_proj, ALU.add).then_inc(s_res, 1)

            def normalise(h, c):
                norm_now, norm3_now = runs(h, c, 4), not own and runs(h, c, -2)
                if norm_now or norm3_now:
                    n = TURN * h + (c + 4 + base)
                    nc.vector.wait_ge(s_rstd, n + 1)
                    nc.vector.wait_ge(s_mv, n + 1)
                    if norm_now:
                        wait(nc.vector, s_xTraw, n - 1)
                        nc.vector.tensor_scalar(xn[:, c % 2, :], x_of(TURN * h + (c + 4)), mean_var[:, 0, 0:1], rstd[:, 0:1],
                                                    ALU.subtract, ALU.mult).then_inc(s_xn, 1)
                    if norm3_now:
                        wait(nc.vector, s_rows, TURN * h + (c - 5))
                        nc.vector.tensor_scalar(xn3[:, (c - 2) % 4, :], x_of(TURN * h + (c - 2)), mean_var[:, 1, 0:1], rstd[:, 1:2],
                                                    ALU.subtract, ALU.mult).then_inc(s_xn3, 1)

            def turn_qk(h, c):
                if not runs(h, c, 2):
                    return
                n = TURN * h + (c + 2 + base)
                nc.vector.wait_ge(s_qkraw, n + 1)
                wait(nc.vector, s_spread, n)
                wait(nc.vector, s_grouped, n)
                pq = p_qk[:, :].rearrange("p (t f k) -> p t f k", t=2, f=2)
                nc.vector.tensor_tensor(turned_cos[:, :, :], pq[:, 0], cv(C_COS, 2 * P).rearrange("p (f k) -> p f k", f=2), ALU.mult)
                nc.vector.tensor_tensor(turned_sin[:, :, :], pq[:, 1], cv(C_SIN, 2 * P).rearrange("p (f k) -> p f k", f=2), ALU.mult).then_inc(s_rot, 1)
                nc.vector.wait_ge(s_rot, n + 1)
                nc.vector.tensor_tensor(qk[:, :, :], turned_cos[:, :, :], turned_sin[:, :, :], ALU.add).then_inc(s_qk, 1)

            def dve_step(h, c):
                def at(lead):
                    return TURN * h + (c + lead)

                def count(lead):
                    return TURN * h + (c + lead + base)
                if own and not runs(h, c, 1):
                    normalise(h, c)
                    turn_qk(h, c)
                    add_result(h, c)
                if runs(h, c, 1):
                    n = count(1)
                    for half in range(2):
                        if own and half == 1:
                            normalise(h, c)
                            turn_qk(h, c)
                            add_result(h, c)
                        nc.vector.wait_ge(s_scores, 2 * n + 1 + half)
                        wait(nc.vector, s_shifted, 2 * n - 1 + half)
                        scores = p_scores[half][:, :].rearrange("p (h k) -> p h k", k=WIN)
                        if dve_masks(half):
                            wait(nc.vector, s_probs, 2 * n - 1 + half)
                            nc.vector.tensor_tensor(lowered[:, half * 8:half * 8 + 8, :], scores,
                                                    cv(C_MASKS + kind * WIN, WIN).unsqueeze(1).to_broadcast([P, 8, WIN]), ALU.add).then_inc(s_masked, 1)
                            nc.vector.wait_ge(s_masked, n + 1)
                            scores = lowered[:, half * 8:half * 8 + 8, :]
                        nc.vector.tensor_reduce((peak if own else shift)[:, half * 8:half * 8 + 8], scores, AX.X, ALU.max).then_inc(s_max, 1)
                        if own:
                            nc.vector.wait_ge(s_max, 2 * n + 1 + half)
                            wait(nc.vector, s_probs, 2 * n - 1 + half)
                            nc.vector.tensor_tensor(lowered[:, half * 8:half * 8 + 8, :], scores,
                                                    peak[:, half * 8:half * 8 + 8].unsqueeze(2).to_broadcast([P, 8, WIN]), ALU.subtract).then_inc(s_shifted, 1)
                if not own:
                    normalise(h, c)
                    add_result(h, c)
                    route_dve_bank(h, c)
                    take_values(nc.vector, h, c)
                    route_dve(h, c)
                yield
                if runs(h, c, 0):
                    n = count(0)
                    nc.vector.wait_ge(s_attraw, n + 1)
                    pairs = p_att[:, 0:PAIRS * VC].rearrange("p (m v) -> p m v", v=VC)
                    nc.vector.reciprocal(inv_sum[:, :, :], pairs[:, :, 2 * HD:VC]).then_inc(s_inv, 1)
                    nc.vector.wait_ge(s_inv, n + 1)
                    wait(nc.vector, s_aTraw, n)
                    nc.vector.tensor_tensor(att[:, :].rearrange("p (m t d) -> p m t d", t=2, d=HD),
                                            pairs[:, :, 0:2 * HD].rearrange("p m (t d) -> p m t d", t=2),
                                            inv_sum[:, :, :].unsqueeze(3).to_broadcast([P, PAIRS, 2, HD]), ALU.mult).then_inc(s_att, 1)
                yield
                if runs(h, c, 5) or (not own and runs(h, c, -1)):
                    n = count(5)
                    wait(nc.vector, s_rstd, n)
                    if runs(h, c, 5):
                        if own and isinstance(h, int) and c == -1:
                            nc.vector.wait_ge(s_x[1], 64)
                        plain(nc.vector)
                        nc.vector.bn_stats(stats[:, 0, :], x_of(at(5))).then_inc(s_stats, 1)
                    if not own and runs(h, c, -1):
                        nc.vector.wait_ge(s_res, count(-1) + 1)
                        plain(nc.vector)
                        nc.vector.bn_stats(stats[:, 1, :], x_of(at(-1))).then_inc(s_st3, 1)
                    if runs(h, c, 5):
                        nc.vector.wait_ge(s_stats, n + 1)
                        plain(nc.vector)
                        a = nc.vector.bn_aggr(mean_var[:, 0, :], stats[:, 0, :])
                    if not own and runs(h, c, -1):
                        nc.vector.wait_ge(s_st3, at(-1) + 1)
                        plain(nc.vector)
                        a = nc.vector.bn_aggr(mean_var[:, 1, :], stats[:, 1, :])
                    a.then_inc(s_mv, 1)
            return pe_step, act_step, pool_step, dve_step

        def n_of_self(n):
            return (n.max_val if not isinstance(n, int) else n) <= B

        def n_is_first(n):
            return isinstance(n, int) and n == 0

        CHOOSE_STEPS, PLACE_STEPS = 6, 8

        def choosing(h, c):
            if c % 2 == 0 and runs(h, c, -4):
                return True, TURN // 2 * h + (c - 4) // 2
            return False, None

        def placing(h, c):
            if c % 2 == 1 and runs(h, c, -5):
                return True, TURN // 2 * h + (c - 5) // 2
            return False, None

        def route_pe(h, c):
            n = TURN * h + (c - 3)
            if runs(h, c, -3):
                nc.tensor.wait_ge(s_x3T, n + 1)
                if c % 2 == 0:
                    wait(nc.tensor, s_begun, TURN // 2 * h + (c - 4) // 2)
                else:
                    wait(nc.tensor, s_choose, CHOOSE_STEPS * (TURN // 2 * h + (c - 5) // 2) + 1)
                t = (c - 3) % 2
                nc.tensor.matmul(p_logits[:, t * E:(t + 1) * E], x3T[:, :], gate[:, :], start=True, stop=True).then_inc(s_gate, 1)
            now, pair = placing(h, c)
            if now:
                nc.tensor.wait_ge(s_onehot, pair + 1)
                mm = nc.tensor.matmul(p_place, before_bf[:, :], onehot[:, :, :].rearrange("p g e -> p (g e)"), start=True, stop=False,
                                      skip_group_check=True)
                for g in range(2 * TOPK):
                    mm = nc.tensor.matmul(p_place[:, (g + 1) * E:], ones_bf[:, :],
                                          onehot[:, g:g + 1, :].to_broadcast([P, 2 * TOPK - g, E]), start=False, stop=(g == 2 * TOPK - 1),
                                          skip_group_check=True)
                mm.then_inc(s_placed, 1)

        def route_bank(eng, h, c):
            now, pair = choosing(h, c)
            if now:
                eng.wait_ge(s_choose, CHOOSE_STEPS * pair + 1)
            now, pair = placing(h, c)
            if now:
                eng.wait_ge(s_begun, pair + 1)

        def route_act(h, c):
            if runs(h, c, -2):
                n = TURN * h + (c - 2)
                nc.scalar.wait_ge(s_x3Traw, n + 1)
                wait(nc.scalar, s_gate, n)
                nc.scalar.copy(x3T[:, :], p_x3T).then_inc(s_x3T, 1)

        def fill_rows(h, c):
            if runs(h, c, -4):
                n = TURN * h + (c - 4)
                t = c % 4
                if not isinstance(h, int) or c - 4 >= 4:
                    nc.scalar.wait_ge(s_sent[t], 32 * h + 32 * ((c - 4) // 4))
                nc.scalar.wait_ge(s_xn3, n + 1)
                nc.scalar.copy(row[:, t, :, 0:P], xn3[:, t:t + 1, :].to_broadcast([P, TOPK, P])).then_inc(s_rows, 1)

        def ratio_act(h, c):
            now, pair = choosing(h, c)
            if now:
                nc.scalar.wait_ge(s_choose, CHOOSE_STEPS * pair + 3)
                wait(nc.scalar, s_place, PLACE_STEPS * pair - PLACE_STEPS + 4)
                for t in range(2):
                    a = nc.scalar.activation(ratio[:, t, :], top[:, t, 0:1], ACT.Exp, bias=top[:, t, 1:2], scale=-1.0)
                a.then_inc(s_ratio, 1)

        def route_pool(h, c, tiles):
            for tile in tiles:
                if isinstance(h, int) and not 0 <= tile < B:
                    continue
                t = tile % 4
                nc.gpsimd.wait_ge(s_slot, TURN // 2 * h + tile // 2 + 1)
                nc.gpsimd.wait_ge(s_rows, TURN * h + tile + 1)
                plain(nc.gpsimd)
                for k in range(TOPK):
                    nc.gpsimd.indirect_dma_start(out=sent, out_offset=bass.IndirectOffsetOnAxis(ap=slot_u[:, t, k:k + 1], axis=0),
                                                 in_=row[:, t, k, :], in_offset=None).then_inc(s_sent[t], 16)

        def route_dve_bank(h, c):
            V = nc.vector
            now, pair = choosing(h, c)
            if now:
                V.wait_ge(s_gate, 2 * pair + 2)
                V.tensor_copy(logits[:, :, :], p_logits.rearrange("p (t e) -> p t e", t=2)).then_inc(s_choose, 1)
            now, pair = placing(h, c)
            if now:
                V.wait_ge(s_placed, pair + 1)
                wait(V, s_begun, pair)
                V.tensor_tensor(place[:, :, :], begin[:, :].unsqueeze(1).to_broadcast([P, 2 * TOPK, E]),
                                p_place[:, 0:2 * TOPK * E].rearrange("p (g e) -> p g e", e=E), ALU.add).then_inc(s_place, 1)
                V.wait_ge(s_place, PLACE_STEPS * pair + 1)
                V.tensor_tensor(begin[:, :], begin[:, :], p_total, ALU.add).then_inc(s_begun, 1)

        def route_dve(h, c):
            V = nc.vector
            now, pair = choosing(h, c)
            if now:
                def done(op):
                    op.then_inc(s_choose, 1)

                def needs(j):
                    V.wait_ge(s_choose, CHOOSE_STEPS * pair + j)
                needs(1)
                wait(V, s_ratio, pair)
                plain(V)
                done(V.max(top[:, 0, :], logits[:, 0, :]))
                done(V.max(top[:, 1, :], logits[:, 1, :]))
                needs(3)
                plain(V)
                done(V.max_index(top_at[:, 0, :], top[:, 0, :], logits[:, 0, :]))
                done(V.max_index(top_at[:, 1, :], top[:, 1, :], logits[:, 1, :]))
                needs(5)
                done(V.tensor_copy(top_atf[:, :, :], top_at[:, :, 0:TOPK]))
                needs(6)
                wait(V, s_placed, pair)
                V.tensor_tensor(onehot[:, 0:2 * TOPK, :], cv(C_IOTA, E).unsqueeze(1).to_broadcast([P, 2 * TOPK, E]),
                                top_atf[:, :, :].rearrange("p t k -> p (t k)").unsqueeze(2).to_broadcast([P, 2 * TOPK, E]),
                                ALU.is_equal).then_inc(s_onehot, 1)
            now, pair = placing(h, c)
            if now:
                def done(op):
                    op.then_inc(s_place, 1)

                def needs(j):
                    V.wait_ge(s_place, PLACE_STEPS * pair + j)
                V.wait_ge(s_ratio, pair + 1)
                done(V.tensor_scalar(ratio1[:, :, :], ratio[:, :, :], 1.0, None, ALU.add))
                half = slice((c - 5) % 4, (c - 5) % 4 + 2)
                if not isinstance(h, int) or c - 5 >= 4:
                    for t in range(half.start, half.stop):
                        V.wait_ge(s_sent[t], 32 * h + 32 * ((c - 5) // 4))
                needs(2)
                done(V.reciprocal(row[:, half, 0, P:P + 1], ratio1[:, :, :]))
                needs(3)
                done(V.tensor_tensor(row[:, half, 1, P:P + 1], row[:, half, 0, P:P + 1], ratio[:, :, :], ALU.mult))
                needs(1)
                V.wait_ge(s_onehot, pair + 1)
                done(V.tensor_tensor(mine[:, :, :], place[:, :, :], onehot[:, 0:2 * TOPK, :], ALU.mult))
                done(V.tensor_copy(row[:, half, :, P + 1:P + 2].squeeze(3), result_no[:, :, :]))
                needs(5)
                done(V.tensor_reduce(slot_f[:, :], mine[:, :, :], AX.X, ALU.add))
                needs(6)
                done(V.tensor_scalar(result_no[:, :, :], result_no[:, :, :], float(2 * P), None, ALU.add))
                needs(8)
                V.tensor_copy(slot_u[:, half, :].rearrange("p t k -> p (t k)"), slot_f[:, :]).then_inc(s_slot, 1)

        def route_table():
            V = nc.vector
            count = [0]

            def chain(op):
                op.then_inc(s_table, 1)
                count[0] += 1
                V.wait_ge(s_table, count[0])
            taken = begin[:, :]
            V.wait_ge(s_begun, B // 2)
            V.tensor_copy(region_end[:, :], taken).then_inc(s_pads, 1)
            chain(V.tensor_tensor(nblocks[:, :], taken, cv(C_REGION, E), ALU.subtract))
            chain(V.tensor_scalar(count_i[:, :], nblocks[:, :], float(P - 1), None, ALU.add))
            chain(V.tensor_scalar(nblocks_i[:, :], count_i[:, :], 7, None, ALU.arith_shift_right))
            chain(V.tensor_copy(ends[:, 0, :], nblocks_i[:, :]))
            for s_, step in enumerate((1, 2, 4)):
                V.tensor_copy(ends[:, s_ + 1, 0:step], ends[:, s_, 0:step])
                chain(V.tensor_tensor(ends[:, s_ + 1, step:E], ends[:, s_, step:E], ends[:, s_, 0:E - step], ALU.add))
            chain(V.tensor_scalar(skip[:, :], ends[:, 0, :], -float(P), float(CAP), ALU.mult, ALU.add))
            number = consts[:, C_ROWNO:C_ROWNO + 1]
            chain(V.tensor_tensor(past[:, 0, :], number.to_broadcast([P, E]), ends[:, 3, :], ALU.is_ge))
            V.tensor_tensor(past[:, 1, :], past[:, 0, :], skip[:, :], ALU.mult).then_inc(s_table, 1)
            count[0] += 1
            V.wait_ge(s_table, count[0])
            chain(V.tensor_reduce(block_sum[:, :], past[:, :, :], AX.X, ALU.add))
            V.tensor_scalar(block_f[:, 0:1], block_sum[:, 0:1], float(E - 1), float(F), ALU.min, ALU.mult).then_inc(s_table, 1)
            count[0] += 1
            chain(V.scalar_tensor_tensor(out=block_f[:, 1:2], in0=number, scalar=float(P), in1=block_sum[:, 1:2], op0=ALU.mult, op1=ALU.add))
            V.tensor_scalar(block_f[:, 1:2], block_f[:, 1:2], float(E * CAP), None, ALU.min).then_inc(s_block, 1)
            V.wait_ge(s_blockT, 1)
            V.tensor_copy(block_tab[0:1, :, :], p_block[0:1, :].rearrange("p (w b) -> p w b", w=2)[:, :, 0:BLOCKS]).then_inc(s_tab, 1)

        def table_pe():
            nc.tensor.wait_ge(s_block, 1)
            for which in range(2):
                mm = nc.tensor.matmul(p_block[0:1, which * P:(which + 1) * P], block_f[:, which:which + 1], ident, start=True, stop=True)
            mm.then_inc(s_blockT, 1)

        LEAD = 6

        def expert_steps(eng, step):
            loop_from = U + 1
            turns = (BLOCKS - LEAD - loop_from) // U
            cols = {}
            for c in range(-2, loop_from):
                step(0, c, cols)
            with eng.Fori(0, turns) as h:
                cols = {}
                for c in range(loop_from, loop_from + U):
                    step(h, c, cols)
            cols = {}
            for c in range(loop_from + U * turns, BLOCKS + 1):
                step(0, c, cols)

        def block_there(h, c, lead):
            return not isinstance(h, int) or 0 <= c + lead < BLOCKS

        def table_at(which, i):
            return block_tab[0:1, which, bass.ds(i, 1)]

        def expert_pe(h, c, _):
            n = U * h + c
            if block_there(h, c, 0):
                half = c % 2
                nc.tensor.wait_ge(s_gT, n + 1)
                nc.tensor.wait_ge(s_w1_now, n + 1)
                wait(nc.tensor, s_gelu, n - 1)
                for f in range(FC):
                    mm = nc.tensor.matmul(p_hidden[half][:, f * P:(f + 1) * P], w1_now[:, half, f * P:(f + 1) * P], gotT[:, half, :],
                                          start=True, stop=True)
                mm.then_inc(s_up, 1)
            if block_there(h, c, -1):
                half = (c - 1) % 2
                nc.tensor.wait_ge(s_gelu, n)
                nc.tensor.wait_ge(s_w2_now, n)
                wait(nc.tensor, s_y, n - 2)
                for f in range(FC):
                    mm = nc.tensor.matmul(p_y[half], hidden[:, half, f * P:(f + 1) * P], w2_now[:, half, f * P:(f + 1) * P],
                                          start=(f == 0), stop=(f == FC - 1))
                mm.then_inc(s_down, 1)
            if block_there(h, c, 2):
                nc.tensor.wait_ge(s_got[(c + 2) % U], 16 * h + 16 * ((c + 2) // U + 1))
                wait(nc.tensor, s_gT, n + 1)
                nc.tensor.transpose(p_gotT[c % 2], got[:, (c + 2) % U, 0:P], ident).then_inc(s_gTraw, 1)

        def first_row(i):
            return nc.scalar.value_load(table_at(1, i), min_val=0, max_val=E * CAP)

        def read_rows(h, c, lead, first=None):
            slot = (c + lead) % U
            n = U * h + (c + lead)
            if not isinstance(h, int) or c + lead >= U:
                nc.scalar.wait_ge(s_y, n + 1 - U)
            if first is None:
                first = first_row(n)
            nc.scalar.dma_start(got[:, slot, :], sent[bass.ds(first, P), :]).then_inc(s_got[slot], 16)

        def expert_act(h, c, _):
            n = U * h + c
            if isinstance(h, int) and c <= 0:
                if c == -2:
                    firsts = [first_row(i) for i in range(3)]
                    for t in range(4):
                        nc.scalar.wait_ge(s_sent[t], 16 * TOPK * B // 4)
                    nc.scalar.wait_ge(s_padsent, 16 * (E + 1))
                    for i in range(3):
                        read_rows(0, 0, i, firsts[i])
                else:
                    for i in range(2 * c + 5, 2 * c + 7):
                        read_rows(0, 0, i)
            elif block_there(h, c, LEAD):
                read_rows(h, c, LEAD)
            if block_there(h, c, 0):
                half = c % 2
                nc.scalar.wait_ge(s_up, n + 1)
                wait(nc.scalar, s_down, n - 1)
                nc.scalar.activation(hidden[:, half, :], p_hidden[half][:, :], ACT.Gelu).then_inc(s_gelu, 1)
            if block_there(h, c, 2):
                nc.scalar.wait_ge(s_gTraw, n + 3)
                nc.scalar.copy(gotT[:, c % 2, :], p_gotT[c % 2]).then_inc(s_gT, 1)

        def expert_dve(h, c, cols):
            n = U * h + c

            def col(lead):
                if c + lead not in cols:
                    cols[c + lead] = nc.vector.value_load(table_at(0, n + lead), min_val=0, max_val=(E - 1) * F)
                return cols[c + lead]
            if block_there(h, c, 2):
                at = col(2)
                wait(nc.vector, s_up, n + 1)
                nc.vector.tensor_copy(w1_now[:, c % 2, :], w1[:, bass.ds(at, F)]).then_inc(s_w1_now, 1)
            if block_there(h, c, -1):
                slot = (c - 1) % U
                nc.vector.wait_ge(s_down, n)
                if not isinstance(h, int) or c - 1 >= U:
                    nc.vector.wait_ge(s_back[slot], 16 * h + 16 * ((c - 1) // U))
                nc.vector.wait_ge(s_got[slot], 16 * h + 16 * ((c - 1) // U + 1))
                nc.vector.tensor_copy(result_at[:, slot:slot + 1], got[:, slot, P + 1:P + 2])
                nc.vector.tensor_scalar(weighted[:, slot, :], p_y[(c - 1) % 2], got[:, slot, P:P + 1], None, ALU.mult).then_inc(s_y, 1)
            if block_there(h, c, 1):
                at = col(1)
                wait(nc.vector, s_down, n)
                nc.vector.tensor_copy(w2_now[:, (c + 1) % 2, :], w2[:, bass.ds(at, F)]).then_inc(s_w2_now, 1)

        def expert_pool(h, c, _):
            n = U * h + c
            if block_there(h, c, -1):
                slot = (c - 1) % U
                nc.gpsimd.wait_ge(s_y, n)
                plain(nc.gpsimd)
                nc.gpsimd.indirect_dma_start(out=results, out_offset=bass.IndirectOffsetOnAxis(ap=result_at[:, slot:slot + 1], axis=0),
                                             in_=weighted[:, slot, :], in_offset=None,
                                             bounds_check=TOPK * TOKENS - 1, oob_is_err=False).then_inc(s_back[slot], 16)

        kinds = [attention(0), attention(1)]

        @block.tensor
        def _(pe):
            pe.wait_ge(s_consts, 16)
            pe.wait_ge(s_wself, 16)
            pe.wait_ge(s_const, 8)
            pe.wait_ge(s_zero, 4)
            attend(pe, kinds[0][0], kinds[1][0])
            pe.wait_ge(s_slot, B // 2)
            table_pe()
            expert_steps(pe, expert_pe)

        @block.scalar
        def _(act):
            act.dma_start(consts[:, :], consts_in).then_inc(s_consts, 16)
            act.dma_start(wcross[:, :], wcross_in).then_inc(s_w, 16)
            act.dma_start(cols[:, :], cols_in).then_inc(s_w, 16)
            act.dma_start(rows[:, :], rows_in.partition_broadcast(P)).then_inc(s_w, 16)
            act.dma_start(gate[:, :], gate_in).then_inc(s_w, 16)
            attend(act, kinds[0][1], kinds[1][1])
            nc.scalar.activation(hidden[0:1, 0, 0:1], eps[0:1, 0:1], ACT.Gelu)
            send_pads(act, range(E // 2, E))
            act.wait_ge(s_tab, 1)
            expert_steps(act, expert_act)

        @block.gpsimd
        def _(pool):
            nc.gpsimd.memset(k_heads[:, :, :], 0.0).then_inc(s_zero, 1)
            pool.wait_ge(s_consts, 16)
            pool.wait_ge(s_const, 8)
            pool.wait_ge(s_zero, 4)
            attend(pool, kinds[0][2], kinds[1][2])
            expert_steps(pool, expert_pool)
            add_results(pool, nc.gpsimd, POOL_CHUNKS, s_sum_pool)

        @block.vector
        def _(dve):
            nc.vector.memset(eps[:, :], EPS).then_inc(s_const, 1)
            nc.vector.memset(minus_half[:, :], -0.5).then_inc(s_const, 1)
            nc.vector.memset(ones_bf[:, :], 1.0).then_inc(s_const, 1)
            nc.vector.memset(onehot[:, 2 * TOPK:, :], 0.0).then_inc(s_const, 1)
            nc.vector.memset(values[:, :, :, :, :], 0.0).then_inc(s_zero, 1)
            dve.wait_ge(s_zero, 2)
            every = values[:, :, :, :, :].rearrange("p s j m v -> p (s j m) v")
            nc.vector.memset(every[0:WIN, :, 2 * HD:2 * HD + 1], 1.0).then_inc(s_zero, 1)
            nc.vector.memset(every[WIN:P, :, 2 * HD + 1:VC], 1.0).then_inc(s_zero, 1)
            nc.vector.memset(mean_var[:, :, :], 1.0)
            nc.vector.memset(row[:, :, :, P + 2:ROW], 0.0)
            nc.vector.memset(pad_row[:, :], 0.0).then_inc(s_pads, 1)
            dve.wait_ge(s_consts, 16)
            nc.vector.tensor_copy(ident_bf[:, :], ident).then_inc(s_const, 1)
            nc.vector.tensor_scalar(minus_ident_bf[:, :], ident, -1.0, None, ALU.mult).then_inc(s_const, 1)
            nc.vector.tensor_copy(masks_bf[:, :], cv(C_MASKS, 2 * WIN)).then_inc(s_const, 1)
            nc.vector.tensor_copy(before_bf[:, :], cv(C_BEFORE, P)).then_inc(s_const, 1)
            nc.vector.tensor_copy(begin[:, :], cv(C_REGION, E)).then_inc(s_const, 1)
            rowno = consts[:, C_ROWNO:C_ROWNO + 1]
            for t in range(2):
                for k in range(TOPK):
                    nc.vector.tensor_scalar(result_no[:, t, k:k + 1], rowno, float(k * TOKENS + t * P), None, ALU.add).then_inc(s_const, 1)
            dve.wait_ge(s_pads, 1)
            nc.vector.tensor_scalar(pad_row[:, P + 1:P + 2], rowno, float(TOPK * TOKENS), None, ALU.add).then_inc(s_pads, 1)
            dve.wait_ge(s_const, 13)
            dve.wait_ge(s_x[0], 16)
            attend(dve, kinds[0][3], kinds[1][3])
            route_table()
            dve.wait_ge(s_moe_w, 32)
            dve.wait_ge(s_tab, 1)
            expert_steps(dve, expert_dve)
            add_results(dve, nc.vector, DVE_CHUNKS, s_sum)


def laid_out(i):
    f = lambda a: np.asarray(a)
    qkv, wo = f(i["L0_attn_w_qkv"]), f(i["L0_attn_w_out"])
    half = np.arange(P).reshape(HEADS, 2, HD // 2)[:, ::-1].reshape(-1)
    q, k, v = qkv[0:P], qkv[P:2 * P], qkv[2 * P:]
    order = np.concatenate([np.arange(b * BLK, (b + 1) * BLK) for b in BLOCK_ORDER])
    c = np.ascontiguousarray
    return {
        "x_in": c(f(i["x"])),
        "ctxT_in": c(f(i["ctx_1024"])[:, order].transpose(0, 2, 1)),
        "consts_in": shape_constants(),
        "wself_in": c(np.concatenate([q.T, q[half].T, k.T, k[half].T, v.T, wo.T], axis=1)),
        "wcross_in": c(np.concatenate([f(i["L0_xattn_W" + s]).T for s in "qkvo"], axis=1)),
        "cols_in": c(np.stack([f(i["L0_xattn_bq"]), f(i["L0_xattn_bk"])], axis=1)),
        "rows_in": c(np.concatenate([f(i["L0_xattn_bv"]), f(i["L0_xattn_bo"])])),
        "gate_in": c(f(i["L0_ffn_gate_w"])),
        "w1_in": c(f(i["L0_ffn_w1"]).transpose(1, 0, 2).reshape(P, E * F)),
        "w2_in": c(f(i["L0_ffn_w2"]).reshape(E, FC, P, P).transpose(2, 0, 1, 3).reshape(P, E * F)),
    }


def kernel(**inputs):
    import concourse.bacc as _bacc
    from concourse.bass_utils import run_bass_kernel_spmd as _run

    nc = _bacc.Bacc("TRN2", target_bir_lowering=False, num_devices=1)
    arrays = laid_out(inputs)
    args = [nc.dram_tensor(n, a.shape, mybir.dt.from_np(a.dtype), kind="ExternalInput").ap() for n, a in arrays.items()]
    out = nc.dram_tensor("out", (B, P, P), mybir.dt.float32, kind="ExternalOutput").ap()
    build(nc, *args, out)
    r = _run(nc, [arrays], core_ids=[0])
    return r.results[0]["out"]
```
